# Optimizing a Trainium2 kernel written in Bass

```python
import numpy as np
import jax
import jax.numpy as jnp

def _softmax(x, axis=-1):
    return jax.nn.softmax(x, axis=axis)

def _gelu(x):
    return jax.nn.gelu(x, approximate=True)

def _silu(x):
    return jax.nn.silu(x)

def _sigmoid(x):
    return jax.nn.sigmoid(x)

def _layernorm(x, axis=-1, eps=1e-05):
    m = jnp.mean(x, axis=axis, keepdims=True)
    v = jnp.var(x, axis=axis, keepdims=True)
    return (x - m) / jnp.sqrt(v + eps)

def _scatter_add(tgt, idx, src, axis=0):
    return tgt.at[idx].add(src)

def _segment_sum(src, seg, n):
    return jax.ops.segment_sum(src, seg, n)
kernel_name = 'mk_seq_postln_d1_jaxref_r8_7b13cb'

def setup_inputs(seed: int=0):
    np.random.seed(seed)
    _w = jnp.asarray

    def _L0_attn_setup():
        import jax, jax.numpy as jnp
        import numpy as np
        B, S, HID = (1, 256, 512)
        NH, NKV = (32, 8)
        HD = HID // NH
        GROUPS = NH // NKV
        ROPE_THETA = 10000.0

        def _rope_cos_sin(seq_len, head_dim, dtype=jnp.float32):
            inv_freq = 1.0 / ROPE_THETA ** (jnp.arange(0, head_dim, 2, dtype=jnp.float32) / head_dim)
            t = jnp.arange(seq_len, dtype=jnp.float32)
            freqs = jnp.outer(t, inv_freq)
            emb = jnp.concatenate([freqs, freqs], axis=-1)
            return (jnp.cos(emb).astype(dtype), jnp.sin(emb).astype(dtype))

        def _rotate_half(x):
            x1, x2 = jnp.split(x, 2, axis=-1)
            return jnp.concatenate([-x2, x1], axis=-1)

        def _apply_rope(x, cos, sin):
            return x * cos[None, None] + _rotate_half(x) * sin[None, None]
        key = jax.random.key(seed)
        k1, k2, k3, k4, k5 = jax.random.split(key, 5)
        return {'hidden_states': jax.random.normal(k1, (B, S, HID), jnp.float32), 'Wq': jax.random.normal(k2, (NH * HD, HID), jnp.float32) * 0.02, 'Wk': jax.random.normal(k3, (NKV * HD, HID), jnp.float32) * 0.02, 'Wv': jax.random.normal(k4, (NKV * HD, HID), jnp.float32) * 0.02, 'Wo': jax.random.normal(k5, (HID, NH * HD), jnp.float32) * 0.02}
    _L0_attn_in = _L0_attn_setup()

    def _L0_ffn_setup():
        import jax, jax.numpy as jnp
        import numpy as np
        HID, INTER = (512, 1792)
        B, S = (2, 256)

        def _binary_diff_weight(w, base):
            d = w - base
            coeff = jnp.mean(jnp.abs(d))
            return base + coeff * jnp.sign(d)
        key = jax.random.key(seed)
        ks = jax.random.split(key, 7)
        return {'hidden_states': jax.random.normal(ks[0], (B, S, HID), dtype=jnp.float32), 'w1': jax.random.normal(ks[1], (INTER, HID), dtype=jnp.float32) * 0.02, 'mean_w1': jax.random.normal(ks[2], (INTER, HID), dtype=jnp.float32) * 0.02, 'w2': jax.random.normal(ks[3], (HID, INTER), dtype=jnp.float32) * 0.02, 'mean_w2': jax.random.normal(ks[4], (HID, INTER), dtype=jnp.float32) * 0.02, 'w3': jax.random.normal(ks[5], (INTER, HID), dtype=jnp.float32) * 0.02, 'mean_w3': jax.random.normal(ks[6], (INTER, HID), dtype=jnp.float32) * 0.02}
    _L0_ffn_in = _L0_ffn_setup()
    _d = {'L0_attn_hidden_states': _L0_attn_in['hidden_states'], 'L0_attn_Wq': _L0_attn_in['Wq'], 'L0_attn_Wk': _L0_attn_in['Wk'], 'L0_attn_Wv': _L0_attn_in['Wv'], 'L0_attn_Wo': _L0_attn_in['Wo'], 'L0_ffn_w1': _L0_ffn_in['w1'], 'L0_ffn_mean_w1': _L0_ffn_in['mean_w1'], 'L0_ffn_w2': _L0_ffn_in['w2'], 'L0_ffn_mean_w2': _L0_ffn_in['mean_w2'], 'L0_ffn_w3': _L0_ffn_in['w3'], 'L0_ffn_mean_w3': _L0_ffn_in['mean_w3']}
    _x0 = _d['L0_attn_hidden_states']
    _d['L0_attn_hidden_states'] = jax.random.normal(jax.random.fold_in(jax.random.key(seed), 1), (4, 512, 512), dtype=_x0.dtype)
    del _x0
    return _d

def reference(L0_attn_hidden_states, L0_attn_Wq, L0_attn_Wk, L0_attn_Wv, L0_attn_Wo, L0_ffn_w1, L0_ffn_mean_w1, L0_ffn_w2, L0_ffn_mean_w2, L0_ffn_w3, L0_ffn_mean_w3):

    def _L0_attn_ref(hidden_states, Wq, Wk, Wv, Wo):
        import jax, jax.numpy as jnp
        import numpy as np
        B, S, HID = (1, 256, 512)
        NH, NKV = (32, 8)
        HD = HID // NH
        GROUPS = NH // NKV
        ROPE_THETA = 10000.0

        def _rope_cos_sin(seq_len, head_dim, dtype=jnp.float32):
            inv_freq = 1.0 / ROPE_THETA ** (jnp.arange(0, head_dim, 2, dtype=jnp.float32) / head_dim)
            t = jnp.arange(seq_len, dtype=jnp.float32)
            freqs = jnp.outer(t, inv_freq)
            emb = jnp.concatenate([freqs, freqs], axis=-1)
            return (jnp.cos(emb).astype(dtype), jnp.sin(emb).astype(dtype))

        def _rotate_half(x):
            x1, x2 = jnp.split(x, 2, axis=-1)
            return jnp.concatenate([-x2, x1], axis=-1)

        def _apply_rope(x, cos, sin):
            return x * cos[None, None] + _rotate_half(x) * sin[None, None]
        bsz, q_len, _ = hidden_states.shape
        q = (hidden_states @ Wq.T).reshape(bsz, q_len, NH, HD).transpose(0, 2, 1, 3)
        k = (hidden_states @ Wk.T).reshape(bsz, q_len, NKV, HD).transpose(0, 2, 1, 3)
        v = (hidden_states @ Wv.T).reshape(bsz, q_len, NKV, HD).transpose(0, 2, 1, 3)
        cos, sin = _rope_cos_sin(q_len, HD, hidden_states.dtype)
        q = _apply_rope(q, cos, sin)
        k = _apply_rope(k, cos, sin)
        k = jnp.repeat(k, GROUPS, axis=1)
        v = jnp.repeat(v, GROUPS, axis=1)
        scale = 1.0 / jnp.sqrt(jnp.asarray(HD, hidden_states.dtype))
        logits = jnp.einsum('bhqd,bhkd->bhqk', q, k) * scale
        causal = jnp.tril(jnp.ones((q_len, q_len), dtype=bool))
        logits = jnp.where(causal[None, None], logits, jnp.finfo(logits.dtype).min)
        attn = jax.nn.softmax(logits, axis=-1)
        out = jnp.einsum('bhqk,bhkd->bhqd', attn, v)
        out = out.transpose(0, 2, 1, 3).reshape(bsz, q_len, NH * HD)
        return out @ Wo.T

    def _L0_ffn_ref(hidden_states, w1, mean_w1, w2, mean_w2, w3, mean_w3):
        import jax, jax.numpy as jnp
        import numpy as np
        HID, INTER = (512, 1792)
        B, S = (2, 256)

        def _binary_diff_weight(w, base):
            d = w - base
            coeff = jnp.mean(jnp.abs(d))
            return base + coeff * jnp.sign(d)
        W1 = _binary_diff_weight(w1, mean_w1)
        W2 = _binary_diff_weight(w2, mean_w2)
        W3 = _binary_diff_weight(w3, mean_w3)
        gate = jnp.einsum('bsh,ih->bsi', hidden_states, W1)
        up = jnp.einsum('bsh,ih->bsi', hidden_states, W3)
        h = jax.nn.silu(gate) * up
        return jnp.einsum('bsi,hi->bsh', h, W2)
    x = L0_attn_hidden_states
    x = _layernorm(x + _L0_attn_ref(x, L0_attn_Wq, L0_attn_Wk, L0_attn_Wv, L0_attn_Wo), axis=-1)
    x = _layernorm(x + _L0_ffn_ref(x, L0_ffn_w1, L0_ffn_mean_w1, L0_ffn_w2, L0_ffn_mean_w2, L0_ffn_w3, L0_ffn_mean_w3), axis=-1)
    return x

_drawn_inputs = setup_inputs


def setup_inputs(seed=0):
    import zlib

    import numpy as np

    out = dict(_drawn_inputs(seed))
    spreads = {}
    factors = {'L0_attn_Wq': 8.0, 'L0_attn_Wk': 8.0}
    for name, (base, spread) in spreads.items():
        noise = np.random.default_rng([zlib.crc32(name.encode()), seed]).standard_normal(out[name].shape)
        drawn = base * np.exp(spread * noise) if base else spread * noise
        out[name] = jnp.asarray(drawn.astype(out[name].dtype))
    for name, factor in factors.items():
        out[name] = (out[name] * factor).astype(out[name].dtype)
    return out
```

```python
from contextlib import ExitStack

import numpy as np
import concourse.bass as bass
from concourse import mybir

F32 = mybir.dt.float32
F32R = mybir.dt.float32r
BF16 = mybir.dt.bfloat16
ALU = mybir.AluOpType
ACT = mybir.ActivationFunctionType
AX_X = mybir.AxisListType.X

P = 128
B, S, D = 4, 512, 512
NH, NKV, HD = 32, 8, 16
GH = NH // NKV
F = 1792
KT = D // P
QT = S // P
NT = F // P
SCALE = float(HD) ** -0.5
EPS = 1e-5
MASKED = -3.0e38

ROWS = 6 * HD
Q_PARTS = (0, 0, 1, 1, 0, 2)
K_PARTS = (0, 1, 0, 1, 2, 0)

U1 = [(0, 0, 4), (1, 0, 2), (1, 2, 2)] + [(t, h, 1) for t in (2, 3) for h in range(GH)]
U2 = [(t, h, 1) for t in (0, 1) for h in range(GH)] + [(2, 0, 2), (2, 2, 2), (3, 0, 4)]
NU = len(U1)
LAST2 = [max(n for n, u in enumerate(U2) if u[0] == t) for t in range(QT)]
LAG = 2
STEPS = NKV + LAG

G_ATT, G_QKV, G_WO = NKV, 8, QT
G_BATCH = G_ATT + G_QKV + G_WO
QKV_USES = (("r", 4), ("v", 5), ("r", 0), ("t", 0), ("t", 1), ("r", 1), ("r", 2), ("r", 3))
N_ROPE = 5
BANK_P1, BANK_P2, BANK_O, BANK_G = 0, 2, 4, 6
NCO = NT


def hold(eng, semaphore, value, passed):
    eng.wait_ge(semaphore, value)
    eng.sem_inc(passed, 1)


def layer(nc, xt, x, wqkv, wo, wall, cos, sin, ident, identf, mask, out):
    with ExitStack() as top:
        def sem(name):
            return top.enter_context(nc.semaphore(name))

        raw_in = sem("raw_in")
        xn_in = sem("xn_in")
        ready0 = sem("ready0")
        wsplit = sem("wsplit")
        xt_in = [sem(f"xt_in{i}") for i in range(2)]
        xsplit = sem("xsplit")
        g_done = sem("g_done")
        g_free = sem("g_free")
        added = sem("added")
        hi_out = sem("hi_out")
        rest = sem("rest")
        mid_out = sem("mid_out")
        lo_out = sem("lo_out")
        stack_in = [sem(f"stack_in{i}") for i in range(N_ROPE)]
        p1_done = sem("p1_done")
        p1_free = sem("p1_free")
        max_split = sem("max_split")
        max_in = sem("max_in")
        p2_done = sem("p2_done")
        exped = sem("exped")
        pv_done = sem("pv_done")
        o_out = sem("o_out")
        o_in = sem("o_in")
        o_norm = sem("o_norm")
        o_split = sem("o_split")
        co_in = [sem(f"co_in{i}") for i in range(2)]
        co_diff = sem("co_diff")
        co_abs = sem("co_abs")
        var_out = sem("var_out")
        std_out = sem("std_out")
        x1_out = sem("x1_out")
        chain = sem("chain")
        coef_ps = sem("coef_ps")
        coef_out = sem("coef_out")
        t_done = sem("t_done")
        t_high = sem("t_high")
        t_out = sem("t_out")
        w_in = [sem(f"w_in{i}") for i in range(2)]
        w_diff = sem("w_diff")
        w_sign = sem("w_sign")
        w_out = sem("w_out")
        gu_done = sem("gu_done")
        sig_out = sem("sig_out")
        h_out = sem("h_out")
        y_done = sem("y_done")
        y_free = sem("y_free")
        fchain = sem("fchain")
        var2_out = sem("var2_out")
        std2_out = sem("std2_out")
        stored = sem("stored")
        passed = sem("passed")

        PS = top.enter_context(nc.psum_tensor("PS", [P, 8, 512], F32))
        y = top.enter_context(nc.sbuf_tensor("y", [P, B * QT, D], F32))
        idf = top.enter_context(nc.sbuf_tensor("idf", [P, P], F32))
        asum = top.enter_context(nc.sbuf_tensor("asum", [P, 3, NCO], F32))
        csum = top.enter_context(nc.sbuf_tensor("csum", [P, 4], F32))
        coef = top.enter_context(nc.sbuf_tensor("coef", [P, 4], F32))
        onesf = top.enter_context(nc.sbuf_tensor("onesf", [P, P], F32))
        eps = top.enter_context(nc.sbuf_tensor("eps", [P, 1], F32))
        bnst = top.enter_context(nc.sbuf_tensor("bnst", [P, QT, 6], F32))
        mv = top.enter_context(nc.sbuf_tensor("mv", [P, QT, 2], F32))
        sd = top.enter_context(nc.sbuf_tensor("sd", [P, QT], F32))
        rs = top.enter_context(nc.sbuf_tensor("rs", [P, QT], F32))

        with ExitStack() as ctx:
            def sb(name, shape, dt):
                return ctx.enter_context(nc.sbuf_tensor(name, shape, dt))

            NC = NH * HD + 2 * NKV * HD
            wqH, wqL = sb("wqH", [P, KT, NC], F32R), sb("wqL", [P, KT, NC], F32R)
            woH, woL = sb("woH", [P, KT, D], F32R), sb("woL", [P, KT, D], F32R)
            Qs, Ks = sb("Qs", [P, NH, S], BF16), sb("Ks", [P, NKV, S], BF16)
            V = sb("V", [P, QT, NKV, 2 * HD], F32)
            Pt = sb("Pt", [P, 2, GH, S], F32)
            xH, xL = sb("xH", [P, KT, S], F32R), sb("xL", [P, KT, S], F32R)
            xraw = sb("xraw", [P, 2, S], F32)
            cs, sn = sb("cs", [P, S], F32), sb("sn", [P, S], F32)
            idb, mk = sb("idb", [P, P], BF16), sb("mk", [P, P], BF16)
            parts = sb("parts", [P, 2, 3, S], BF16)
            Oe = sb("Oe", [P, S], F32)
            Oc = sb("Oc", [P, 2, S], F32)
            Dn = sb("Dn", [P, S], F32)
            OH, OL = sb("OH", [P, KT, S], F32R), sb("OL", [P, KT, S], F32R)
            negM = sb("negM", [P, GH, QT], F32)
            negR = sb("negR", [P, GH, QT], F32)
            NM = 3 * GH * QT
            mp_all = sb("mp", [P, P], BF16)
            mp = mp_all[:, 0:NM].rearrange("p (a h t) -> p a h t", a=3, h=GH)
            mT = sb("mT", [NM, P], BF16)
            co = sb("co", [P, 2, 2, 512], F32)
            raw = Qs[:].rearrange("p h s -> p (h s)").bitcast(F32)
            raw_q = raw[:, 0:KT * NC].rearrange("p (k n) -> p k n", k=KT)
            raw_o = raw[:, KT * NC:KT * (NC + D)].rearrange("p (k n) -> p k n", k=KT)

            def g_bank(n):
                return PS[:, BANK_G + n % 2, :]

            def g_att(b):
                return G_QKV + G_BATCH * b

            def g_qkv(b):
                return 0 if isinstance(b, int) and b == 0 else G_BATCH * b - G_WO

            def g_wo(b, last):
                return g_att(b) + G_ATT + (0 if last else G_QKV)

            with nc.Block() as block:

                @block.sync
                def _(sp):
                    for dst, src in ((raw_q, wqkv), (raw_o, wo), (cs[:], cos), (sn[:], sin),
                                     (idb[:], ident), (mk[:], mask), (idf[:], identf)):
                        sp.dma_start(dst, src).then_inc(raw_in, 16)

                    def load_xt(b, k):
                        if not (isinstance(b, int) and b == 0 and k < 2):
                            hold(sp, xsplit, b * KT + k - 1, passed)
                        sp.dma_start(xraw[:, k % 2, :], xt[b, :, k, :]).then_inc(xt_in[k % 2], 16)

                    def load_co(b, c):
                        hold(sp, co_abs, b * NCO + c + 1, passed)
                        sp.dma_start(co[:, c % 2], wall[b, c]).then_inc(co_in[c % 2], 16)

                    def stacks(b):
                        for r in range(N_ROPE):
                            dst, order, h0 = (Ks, K_PARTS, 0) if r == 0 else (Qs, Q_PARTS, 8 * (r - 1))
                            for part, done in ((0, hi_out), (1, mid_out), (2, lo_out)):
                                hold(sp, done, b * N_ROPE + r + 1, passed)
                                for i in range(6):
                                    if order[i] == part:
                                        sp.dma_start(dst[HD * i:HD * (i + 1), h0:h0 + 8, :],
                                                     parts[:, r % 2, part, :]).then_inc(stack_in[r], 16)

                    def max_rows(b, g):
                        hold(sp, g_free, g_att(b) + g + 3, passed)
                        sp.dma_start(Qs[ROWS:ROWS + 3, GH * g:GH * (g + 1), :], mT[:]).then_inc(max_in, 16)

                    def compact(b, g):
                        hold(sp, o_out, b * NKV + g + 3, passed)
                        hold(sp, o_split, b * KT + g // 2 + 1, passed)
                        hold(sp, o_norm, b * KT + g // 2 + 1, passed)
                        for j in range(GH):
                            to = 64 * (g % 2) + HD * j
                            sp.dma_start(Oc[to:to + HD, g // 2 % 2, :], Oe[32 * j:32 * j + HD, :]).then_inc(o_in, 16)
                            sp.dma_start(Dn[to:to + HD, :], Oe[32 * j + HD:32 * j + 2 * HD, :]).then_inc(o_in, 16)

                    def batch(b, last):
                        for s in range(STEPS):
                            if not last:
                                load_co(b, s)
                                if 2 <= s < 2 + KT:
                                    load_xt(b + 1, s - 2)
                            if 1 <= s <= NKV:
                                max_rows(b, s - 1)
                            if s >= LAG + 1:
                                compact(b, s - LAG - 1)
                        compact(b, NKV - 1)
                        if not last:
                            for c in range(STEPS, NCO):
                                load_co(b, c)
                            stacks(b + 1)

                    for k in range(KT):
                        load_xt(0, k)
                    for b in range(B):
                        sp.dma_start(y[:, QT * b:QT * (b + 1), :], x[b]).then_inc(xn_in, 16)
                    stacks(0)
                    with sp.Fori(0, B - 1) as b:
                        batch(b, False)
                    batch(B - 1, True)

                @block.gpsimd
                def _(pool):
                    def rope_add(b, r, n):
                        pool.wait_ge(g_free, n + 3)
                        t = Pt[:, r % 2]
                        pool.tensor_tensor(t[:, 0, :], t[:, 0, :], t[:, 1, :], ALU.add).then_inc(added, 1)

                    def low(b, r):
                        pool.wait_ge(mid_out, b * N_ROPE + r + 1)
                        pool.tensor_tensor(parts[:, r % 2, 2, :], Pt[:, r % 2, 1, :], parts[:, r % 2, 1, :],
                                           ALU.subtract).then_inc(lo_out, 1)

                    def ropes(b):
                        n0 = g_qkv(b)
                        ns = [n0 + e for e, (kind, _) in enumerate(QKV_USES) if kind == "r"]
                        for r in range(N_ROPE):
                            rope_add(b, r, ns[r])
                            low(b, r)

                    def diff(b, c):
                        pool.wait_ge(co_in[c % 2], (b * (NCO // 2) + c // 2 + 1) * 16)
                        pool.tensor_tensor(co[:, c % 2, 0], co[:, c % 2, 0], co[:, c % 2, 1],
                                           ALU.subtract).then_inc(co_diff, 1)

                    def batch(b, last):
                        for s in range(STEPS):
                            if not last:
                                diff(b, s)
                        if not last:
                            for c in range(STEPS, NCO):
                                diff(b, c)
                            ropes(b + 1)

                    ropes(0)
                    with pool.Fori(0, B - 1) as b:
                        batch(b, False)
                    batch(B - 1, True)

                @block.scalar
                def _(act):
                    def high(b, r):
                        act.wait_ge(added, b * N_ROPE + r + 1)
                        if r >= 2:
                            act.wait_ge(stack_in[r - 2], (b + 1) * 96)
                        act.activation(parts[:, r % 2, 0, :], Pt[:, r % 2, 0, :], ACT.Copy).then_inc(hi_out, 1)

                    def middle(b, r):
                        act.wait_ge(rest, b * N_ROPE + r + 1)
                        act.activation(parts[:, r % 2, 1, :], Pt[:, r % 2, 1, :], ACT.Copy).then_inc(mid_out, 1)

                    def ropes(b):
                        for r in range(N_ROPE):
                            high(b, r)
                            middle(b, r)

                    def exp_unit(b, g, n):
                        t, h, m = U2[n]
                        w = S - P * t
                        act.wait_ge(p2_done, (b * NKV + g) * NU + n + 1)
                        if h == 0:
                            act.wait_ge(pv_done, (b * NKV + g) * QT + t + 1)
                        act.activation(Pt[:, t % 2, h:h + m, P * t:S],
                                       PS[:, BANK_P2 + (g * NU + n) % 2, 0:m * w].rearrange("p (m w) -> p m w", m=m),
                                       ACT.Exp, scale=SCALE).then_inc(exped, 1)

                    def o_copy(b, g):
                        act.wait_ge(pv_done, (b * NKV + g + 1) * QT + 2)
                        act.wait_ge(o_in, (b * NKV + g) * 128 + 128)
                        act.activation(Oe[:], PS[:, BANK_O + g % 2, :], ACT.Copy).then_inc(o_out, 1)

                    def abs_sum(b, c):
                        act.wait_ge(co_diff, b * NCO + c + 1)
                        act.activation(co[:, c % 2, 1], co[:, c % 2, 0], ACT.Abs,
                                       accum_out=asum[:, b, c:c + 1]).then_inc(co_abs, 1)

                    def std(b):
                        act.wait_ge(var_out, b + 1)
                        act.activation(sd[:], mv[:, :, 1], ACT.Sqrt, bias=eps[:]).then_inc(std_out, 1)

                    def batch(b, last):
                        for s in range(STEPS):
                            if s < LAG and not last:
                                abs_sum(b, s)
                            if s >= LAG:
                                for n in range(NU):
                                    exp_unit(b, s - LAG, n)
                                    if n == 3 and s > LAG:
                                        o_copy(b, s - LAG - 1)
                                    if n == 7 and not last:
                                        abs_sum(b, s)
                        o_copy(b, NKV - 1)
                        if not last:
                            for c in range(STEPS, NCO):
                                abs_sum(b, c)
                            ropes(b + 1)
                        std(b)

                    ropes(0)
                    with act.Fori(0, B - 1) as b:
                        batch(b, False)
                    batch(B - 1, True)

                @block.vector
                def _(dve):
                    links = [0, 0]
                    rope_base = [0]

                    def split_x(b, k):
                        dve.wait_ge(xt_in[k % 2], (b * 2 + k // 2 + 1) * 16)
                        done = link(dve.tensor_copy(xH[:, k, :], xraw[:, k % 2, :]))
                        dve.wait_ge(chain, done)
                        dve.tensor_tensor(xL[:, k, :], xraw[:, k % 2, :], xH[:, k, :].bitcast(F32),
                                          ALU.subtract).then_inc(xsplit, 1)

                    def link(ins):
                        ins.then_inc(chain, 1)
                        links[1] += 1
                        return links[0] + links[1]

                    def rope_products(r, e, n):
                        ps, t, half = g_bank(e), Pt[:, r % 2], P // 2
                        dve.wait_ge(g_done, n + 1)
                        if r >= 2:
                            dve.wait_ge(lo_out, rope_base[0] + r - 1)
                        dve.tensor_tensor(t[:, 0, :], ps, cs[:], ALU.mult)
                        dve.tensor_tensor(t[0:half, 1, :], ps[half:P, :], sn[0:half, :], ALU.mult)
                        dve.tensor_tensor(t[half:P, 1, :], ps[0:half, :], sn[half:P, :],
                                          ALU.mult).then_inc(g_free, 1)

                    def remainder(b, r):
                        dve.wait_ge(hi_out, b * N_ROPE + r + 1)
                        dve.tensor_tensor(Pt[:, r % 2, 1, :], Pt[:, r % 2, 0, :], parts[:, r % 2, 0, :],
                                          ALU.subtract).then_inc(rest, 1)

                    def qkv(b, before):
                        rope_base[0] = b * N_ROPE
                        n0 = g_qkv(b)
                        r = 0
                        for e, (kind, i) in enumerate(QKV_USES):
                            if kind == "r":
                                rope_products(r, e, n0 + e)
                                if before and r == 0:
                                    normalise(b - 1, KT - 1)
                                remainder(b, r)
                                r += 1
                            elif kind == "v":
                                dve.wait_ge(g_done, n0 + e + 1)
                                dve.tensor_copy(Pt[:, 0, 2, :], g_bank(e)).then_inc(g_free, 1)
                            else:
                                dve.wait_ge(g_done, n0 + e + 1)
                                dve.tensor_copy(V[:, 2 * i:2 * i + 2, :, 0:HD],
                                                g_bank(e)[:, 0:2 * P].rearrange("p (t h d) -> p t h d", t=2, d=HD)
                                                ).then_inc(g_free, 1)

                    def maxima(b, g, n):
                        t, h, m = U1[n]
                        w = P * (t + 1)
                        dve.wait_ge(p1_done, (b * NKV + g) * NU + n + 1)
                        dve.tensor_reduce(negM[:, h:h + m, t],
                                          PS[:, BANK_P1 + (g * NU + n) % 2, 0:m * w].rearrange("p (m w) -> p m w", m=m),
                                          AX_X, ALU.max, negate=True).then_inc(p1_free, 1)

                    def split_max(b, g):
                        dve.wait_ge(p1_free, (b * NKV + g + 1) * NU + 2)
                        a = link(dve.tensor_copy(mp[:, 0], negM[:]))
                        dve.wait_ge(chain, a)
                        a = link(dve.tensor_tensor(negR[:], negM[:], mp[:, 0], ALU.subtract))
                        dve.wait_ge(chain, a)
                        a = link(dve.tensor_copy(mp[:, 1], negR[:]))
                        dve.wait_ge(chain, a)
                        dve.tensor_tensor(mp[:, 2], negR[:], mp[:, 1], ALU.subtract).then_inc(max_split, 1)

                    def max_copy(b, g):
                        dve.wait_ge(g_done, g_att(b) + g + 1)
                        dve.wait_ge(max_in, (b * NKV + g) * 16 + 16)
                        dve.tensor_copy(mT[:], g_bank(g).bitcast(BF16)[0:NM, 0:P]).then_inc(g_free, 1)

                    def normalise(b, k):
                        dve.wait_ge(o_in, (b * KT + k + 1) * 256 + 128)
                        a = link(dve.reciprocal(Dn[:], Dn[:]))
                        dve.wait_ge(chain, a)
                        o = Oc[:, k % 2, :]
                        dve.tensor_tensor(o, o, Dn[:], ALU.mult).then_inc(o_norm, 1)
                        dve.wait_ge(o_norm, b * KT + k + 2)
                        a = link(dve.tensor_copy(OH[:, k, :], o))
                        dve.wait_ge(chain, a)
                        dve.tensor_tensor(OL[:, k, :], o, OH[:, k, :].bitcast(F32), ALU.subtract).then_inc(o_split, 1)

                    def project_out(b, last):
                        n0 = g_wo(b, last)
                        for t in range(QT):
                            yt = y[:, b * QT + t, :]
                            dve.wait_ge(g_done, n0 + t + 1)
                            dve.tensor_tensor(yt, g_bank(t), yt, ALU.add).then_inc(g_free, 1)
                            hold(dve, g_free, n0 + t + 3, passed)
                            a = link(dve.bn_stats(bnst[:, t], yt))
                            hold(dve, chain, a, passed)
                            a = dve.bn_aggr(mv[:, t], bnst[:, t])
                            if t == QT - 1:
                                a.then_inc(var_out, 1)
                        dve.wait_ge(std_out, b + 1)
                        a = link(dve.reciprocal(rs[:], sd[:]))
                        dve.wait_ge(chain, a)
                        for t in range(QT):
                            yt = y[:, b * QT + t, :]
                            dve.tensor_scalar(yt, yt, mv[:, t, 0:1], rs[:, t:t + 1], ALU.subtract,
                                              ALU.mult).then_inc(x1_out, 1)

                    CH_START = 2 + KT
                    CH_BATCH = 3 * NKV + KT + 2 * KT + QT + 1

                    def batch(b, last):
                        links[:] = [b * CH_BATCH + CH_START, 0]
                        for s in range(STEPS):
                            if s < NKV:
                                for n in range(NU):
                                    maxima(b, s, n)
                                    if n == 3 and s >= 1:
                                        max_copy(b, s - 1)
                                split_max(b, s)
                            elif s == NKV:
                                max_copy(b, NKV - 1)
                            if 2 <= s < 2 + KT and not last:
                                split_x(b + 1, s - 2)
                            if s in (5, 7, 9):
                                normalise(b, (s - 5) // 2)
                        if last:
                            normalise(b, KT - 1)
                        else:
                            qkv(b + 1, True)
                        project_out(b, last)
                        if not last:
                            assert links[1] == CH_BATCH

                    dve.memset(V[:], 1.0).then_inc(ready0, 1)
                    dve.memset(Ks[:], 1.0).then_inc(ready0, 1)
                    dve.memset(mp_all[:], 0.0).then_inc(ready0, 1)
                    dve.memset(eps[:], EPS).then_inc(ready0, 1)
                    dve.memset(onesf[:], 1.0).then_inc(ready0, 1)
                    for ring in (g_free, p1_free, exped, pv_done, o_out, o_split, co_abs):
                        dve.sem_inc(ring, 2)
                    for one, full in ((o_norm, 1), (o_in, 128), (max_in, 16)):
                        dve.sem_inc(one, full)
                    dve.wait_ge(raw_in, 7 * 16)
                    for k in range(KT):
                        split_x(0, k)
                    a = link(dve.tensor_copy(wqH[:], raw_q))
                    dve.wait_ge(chain, a)
                    dve.tensor_tensor(wqL[:], raw_q, wqH[:].bitcast(F32), ALU.subtract).then_inc(wsplit, 1)
                    a = link(dve.tensor_copy(woH[:], raw_o))
                    dve.wait_ge(chain, a)
                    dve.tensor_tensor(woL[:], raw_o, woH[:].bitcast(F32), ALU.subtract).then_inc(wsplit, 1)
                    dve.wait_ge(wsplit, 2)
                    dve.wait_ge(xn_in, B * 16)
                    qkv(0, False)
                    assert links == [0, CH_START]
                    with dve.Fori(0, B - 1) as b:
                        batch(b, False)
                    batch(B - 1, True)

                @block.tensor
                def _(pe):
                    def three(dst, stH, stL, moH, moL, k, n):
                        pe.matmul(dst, stH, moH, start=(k == 0), stop=False)
                        pe.matmul(dst, stH, moL, start=False, stop=False)
                        return pe.matmul(dst, stL, moH, start=False, stop=(k == n - 1))

                    def qkv(b):
                        n0 = g_qkv(b)
                        for e, (kind, i) in enumerate(QKV_USES):
                            pe.wait_ge(g_free, n0 + e + 1)
                            if kind == "t":
                                if i == 0:
                                    pe.wait_ge(g_free, n0 + 4)
                                for t in range(2):
                                    m = pe.transpose(g_bank(e)[:, P * t:P * (t + 1)],
                                                     Pt[:, 0, 2, P * (2 * i + t):P * (2 * i + t + 1)], idf[:])
                            else:
                                for k in range(KT):
                                    if e == 0:
                                        pe.wait_ge(xsplit, b * KT + k + 1)
                                    c = slice(P * i, P * (i + 1))
                                    m = three(g_bank(e), wqH[:, k, c], wqL[:, k, c], xH[:, k, :], xL[:, k, :], k, KT)
                            m.then_inc(g_done, 1)

                    def pass1(b, g, n):
                        t, h0, m = U1[n]
                        w = P * (t + 1)
                        bank = PS[:, BANK_P1 + (g * NU + n) % 2, :]
                        pe.wait_ge(p1_free, (b * NKV + g) * NU + n + 1)
                        for i in range(m):
                            pe.matmul(bank[:, i * w:(i + 1) * w], Qs[0:ROWS, GH * g + h0 + i, P * t:P * (t + 1)],
                                      Ks[0:ROWS, g, 0:w], start=True, stop=False)
                            last = pe.matmul(bank[:, (i + 1) * w - P:(i + 1) * w], idb[:], mk[:], start=False, stop=True)
                        last.then_inc(p1_done, 1)

                    def max_transpose(b, g):
                        pe.wait_ge(max_split, b * NKV + g + 1)
                        pe.wait_ge(g_free, g_att(b) + g + 1)
                        pe.transpose(g_bank(g).bitcast(BF16)[:, 0:P], mp_all[:], idb[:]).then_inc(g_done, 1)

                    def pass2(b, g, n):
                        t, h0, m = U2[n]
                        w = S - P * t
                        bank = PS[:, BANK_P2 + (g * NU + n) % 2, :]
                        pe.wait_ge(exped, (b * NKV + g) * NU + n + 1)
                        if n == 0:
                            pe.wait_ge(max_in, (b * NKV + g + 1) * 16 + 16)
                        for i in range(m):
                            pe.matmul(bank[:, i * w:(i + 1) * w], Ks[0:ROWS + 3, g, P * t:P * (t + 1)],
                                      Qs[0:ROWS + 3, GH * g + h0 + i, P * t:S], start=True, stop=False)
                            last = pe.matmul(bank[:, i * w:i * w + P], mk[:], idb[:], start=False, stop=True)
                        last.then_inc(p2_done, 1)

                    def pv(b, g, t):
                        if t == 0:
                            pe.wait_ge(o_out, b * NKV + g + 1)
                        pe.wait_ge(exped, (b * NKV + g) * NU + LAST2[t] + 3)
                        for h in range(GH):
                            last = pe.matmul(PS[32 * h:32 * (h + 1), BANK_O + g % 2, P * t:S], V[:, t, g, :],
                                             Pt[:, t % 2, h, P * t:S], start=(t == 0), stop=(t == QT - 1),
                                             tile_position=(0, 32 * h))
                        last.then_inc(pv_done, 1)

                    def project_out(b, last):
                        n0 = g_wo(b, last)
                        pe.wait_ge(o_split, b * KT + KT + 2)
                        for t in range(QT):
                            pe.wait_ge(g_free, n0 + t + 1)
                            c = slice(P * t, P * (t + 1))
                            for k in range(KT):
                                m = three(g_bank(t), OH[:, k, c], OL[:, k, c], woH[:, k, :], woL[:, k, :], k, KT)
                            m.then_inc(g_done, 1)

                    def batch(b, last):
                        for r in range(N_ROPE):
                            pe.wait_ge(stack_in[r], (b + 1) * 96)
                        for s in range(STEPS):
                            g = s - LAG
                            for n in range(NU):
                                if g >= 0:
                                    pass2(b, g, n)
                                if s < NKV:
                                    pass1(b, s, n)
                                if n == 3 and 1 <= s <= NKV:
                                    max_transpose(b, s - 1)
                                if n == 1 and g >= 1:
                                    pv(b, g - 1, 3)
                                if n == 6 and g >= 0:
                                    pv(b, g, 0)
                                if n == 9 and g >= 0:
                                    pv(b, g, 1)
                            if g >= 0:
                                pv(b, g, 2)
                        pv(b, NKV - 1, 3)
                        if not last:
                            qkv(b + 1)
                        project_out(b, last)

                    pe.wait_ge(ready0, 5)
                    pe.wait_ge(wsplit, 2)
                    qkv(0)
                    with pe.Fori(0, B - 1) as b:
                        batch(b, False)
                    batch(B - 1, True)

        with ExitStack() as ctx:
            def sb(name, shape, dt):
                return ctx.enter_context(nc.sbuf_tensor(name, shape, dt))

            XH, XL = sb("XH", [P, KT, B, S], F32R), sb("XL", [P, KT, B, S], F32R)
            Wr = sb("Wr", [P, 2, 3, 2, 512], F32)
            WH, WL = sb("WH", [P, 2, 3, 512], F32R), sb("WL", [P, 2, 3, 512], F32R)
            sg = sb("sg", [P, 2, S], F32)
            hb, hf = sb("hb", [P, S], F32), sb("hf", [P, S], F32)
            hH, hL = sb("hH", [P, 2, S], F32R), sb("hL", [P, 2, S], F32R)
            BANK_Y = 4
            PAIRS = NT // 2
            UNITS = 2 * B

            with nc.Block() as block:

                @block.sync
                def _(sp):
                    def load(i, par):
                        for t in range(3):
                            sp.dma_start(Wr[:, par, t], wall[t, i]).then_inc(w_in[par], 16)

                    load(0, 0)
                    load(1, 1)
                    with sp.Fori(0, PAIRS - 1) as it:
                        for par in range(2):
                            hold(sp, w_out, it * 6 + 3 * par + 3, passed)
                            load(it * 2 + par + 2, par)
                    for b in range(B):
                        for t in range(QT):
                            sp.wait_ge(x1_out, B * QT + b * QT + t + 1)
                            sp.dma_start(out[b, :, t, :], y[:, b * QT + t, :]).then_inc(stored, 16)
                    sp.wait_ge(stored, B * QT * 16)

                @block.gpsimd
                def _(pool):
                    def diff(it, par):
                        pool.wait_ge(w_in[par], (it + 1) * 48)
                        for t in range(3):
                            w = Wr[:, par, t]
                            pool.tensor_tensor(w[:, 0], w[:, 0], w[:, 1], ALU.subtract).then_inc(w_diff, 1)

                    diff(0, 0)
                    with pool.Fori(0, PAIRS - 1) as it:
                        diff(it, 1)
                        diff(it + 1, 0)
                    diff(PAIRS - 1, 1)

                @block.scalar
                def _(act):
                    def sign(n3, par, t):
                        act.wait_ge(w_diff, n3 + t + 1)
                        act.activation(Wr[:, par, t, 0], Wr[:, par, t, 0], ACT.Sign).then_inc(w_sign, 1)

                    def sigmoid(n, par):
                        act.wait_ge(gu_done, n * 2 + 1)
                        act.wait_ge(h_out, n + 1)
                        act.activation(sg[:, par], PS[:, 2 * par, :], ACT.Sigmoid).then_inc(sig_out, 1)

                    def std(b):
                        act.wait_ge(var2_out, b + 1)
                        act.activation(sd[:], mv[:, :, 1], ACT.Sqrt, bias=eps[:]).then_inc(std2_out, 1)

                    def pair(it, last):
                        for u in range(UNITS):
                            i, b = u // B, u % B
                            if not (last and u == UNITS - 1):
                                sigmoid(it * UNITS + u + 1, (u + 1) % 2)
                            if b < 3 and not (last and i == 1):
                                sign(it * 6 + 3 * i + 3, (i + 1) % 2, b)
                            if last and i == 1:
                                std(b)

                    for n in range(B * KT):
                        act.wait_ge(t_done, n + 1)
                        act.activation(XH[:, n % KT, n // KT, :], PS[:, n % 8, :], ACT.Copy).then_inc(t_high, 1)
                    for t in range(3):
                        sign(0, 0, t)
                    sigmoid(0, 0)
                    with act.Fori(0, PAIRS - 1) as it:
                        pair(it, False)
                    pair(PAIRS - 1, True)

                @block.vector
                def _(dve):
                    links = [0, 0]

                    def link(ins):
                        ins.then_inc(fchain, 1)
                        links[1] += 1
                        return links[0] + links[1]

                    def weights(n3, par, t):
                        dve.wait_ge(w_sign, n3 + t + 1)
                        w = Wr[:, par, t]
                        a = link(dve.scalar_tensor_tensor(out=w[:, 0], in0=w[:, 0], scalar=coef[:, t:t + 1],
                                                          in1=w[:, 1], op0=ALU.mult, op1=ALU.add))
                        dve.wait_ge(fchain, a)
                        a = link(dve.tensor_copy(WH[:, par, t], w[:, 0]))
                        dve.wait_ge(fchain, a)
                        dve.tensor_tensor(WL[:, par, t], w[:, 0], WH[:, par, t].bitcast(F32),
                                          ALU.subtract).then_inc(w_out, 1)

                    def silu(n, par):
                        dve.wait_ge(sig_out, n + 1)
                        a = link(dve.tensor_tensor(hb[:], PS[:, 2 * par, :], sg[:, par], ALU.mult))
                        dve.wait_ge(fchain, a)
                        dve.wait_ge(gu_done, n * 2 + 2)
                        a = link(dve.tensor_tensor(hf[:], PS[:, 2 * par + 1, :], hb[:], ALU.mult))
                        dve.wait_ge(fchain, a)
                        a = link(dve.tensor_copy(hH[:, par], hf[:]))
                        dve.wait_ge(fchain, a)
                        dve.tensor_tensor(hL[:, par], hf[:], hH[:, par].bitcast(F32), ALU.subtract).then_inc(h_out, 1)

                    def accumulate(n, b):
                        for t in range(QT):
                            yt = y[:, b * QT + t, :]
                            dve.wait_ge(y_done, n * QT + t + 1)
                            dve.wait_ge(y_free, n * QT + t + 1)
                            dve.tensor_tensor(yt, PS[:, BANK_Y + t, :], yt, ALU.add).then_inc(y_free, 1)

                    def norm(n, b):
                        for t in range(QT):
                            yt = y[:, b * QT + t, :]
                            dve.wait_ge(y_free, n * QT + t + 17)
                            a = link(dve.bn_stats(bnst[:, t], yt))
                            dve.wait_ge(fchain, a)
                            a = dve.bn_aggr(mv[:, t], bnst[:, t])
                        a.then_inc(var2_out, 1)
                        dve.wait_ge(std2_out, b + 1)
                        a = link(dve.reciprocal(rs[:], sd[:]))
                        dve.wait_ge(fchain, a)
                        for t in range(QT):
                            yt = y[:, b * QT + t, :]
                            dve.tensor_scalar(yt, yt, mv[:, t, 0:1], rs[:, t:t + 1], ALU.subtract,
                                              ALU.mult).then_inc(x1_out, 1)

                    def pair(it, last):
                        links[:] = [it * FCH_PAIR + FCH_START, 0]
                        for u in range(UNITS):
                            i, b, n = u // B, u % B, it * UNITS + u
                            if not (last and u == UNITS - 1):
                                silu(n + 1, (u + 1) % 2)
                            if b < 3 and not (last and i == 1):
                                weights(it * 6 + 3 * i + 3, (i + 1) % 2, b)
                            accumulate(n, b)
                            if last and i == 1:
                                norm(n, b)
                        if not last:
                            assert links[1] == FCH_PAIR

                    FCH_START = 1 + 2 * 3 + 3
                    FCH_PAIR = 3 * UNITS + 2 * 6

                    a = link(dve.tensor_reduce(csum[:, 0:3], asum[:], AX_X, ALU.add))
                    for ring, free in ((h_out, 2), (y_free, 16)):
                        dve.sem_inc(ring, free)
                    for n in range(B * KT):
                        dve.wait_ge(t_high, n + 1)
                        dve.tensor_tensor(XL[:, n % KT, n // KT, :], PS[:, n % 8, :],
                                          XH[:, n % KT, n // KT, :].bitcast(F32), ALU.subtract).then_inc(t_out, 1)
                    dve.wait_ge(coef_ps, 1)
                    dve.tensor_scalar(coef[:, 0:3], PS[:, 0, 0:3], 1.0 / (F * D), None, ALU.mult).then_inc(coef_out, 1)
                    dve.wait_ge(coef_out, 1)
                    for t in range(3):
                        weights(0, 0, t)
                    silu(0, 0)
                    assert links[1] == FCH_START
                    with dve.Fori(0, PAIRS - 1) as it:
                        pair(it, False)
                    pair(PAIRS - 1, True)

                @block.tensor
                def _(pe):
                    def three(dst, stH, stL, moH, moL, k, n):
                        pe.matmul(dst, stH, moH, start=(k == 0), stop=False)
                        pe.matmul(dst, stH, moL, start=False, stop=False)
                        return pe.matmul(dst, stL, moH, start=False, stop=(k == n - 1))

                    def gate_up(n, n3, par, wpar, b):
                        pe.wait_ge(h_out, n + 1)
                        for t in range(2):
                            pe.wait_ge(w_out, n3 + t + 1)
                            for k in range(KT):
                                c = slice(P * k, P * (k + 1))
                                m = three(PS[:, 2 * par + t, :], WH[:, wpar, t, c], WL[:, wpar, t, c],
                                          XH[:, k, b, :], XL[:, k, b, :], k, KT)
                            m.then_inc(gu_done, 1)

                    def down(n, n3, par, wpar):
                        pe.wait_ge(h_out, n + 3)
                        pe.wait_ge(w_out, n3 + 3)
                        for t in range(QT):
                            pe.wait_ge(y_free, n * QT + t + 13)
                            c = slice(P * t, P * (t + 1))
                            three(PS[:, BANK_Y + t, :], hH[:, par, c], hL[:, par, c], WH[:, wpar, 2], WL[:, wpar, 2],
                                  0, 1).then_inc(y_done, 1)

                    def pair(it, last):
                        for u in range(UNITS):
                            i, n, v = u // B, it * UNITS + u, u + 1
                            if v < UNITS:
                                gate_up(n + 1, it * 6 + 3 * (v // B), v % 2, v // B, v % B)
                            elif not last:
                                gate_up(n + 1, it * 6 + 6, 0, 0, 0)
                            down(n, it * 6 + 3 * i, u % 2, i)

                    for n in range(B * KT):
                        if n % KT == 0:
                            pe.wait_ge(x1_out, n + QT)
                        if n >= 8:
                            pe.wait_ge(t_out, n - 7)
                        k, b = n % KT, n // KT
                        for t in range(QT):
                            m = pe.transpose(PS[:, n % 8, P * t:P * (t + 1)], y[:, b * QT + t, P * k:P * (k + 1)], idf[:])
                        m.then_inc(t_done, 1)
                    pe.wait_ge(fchain, 1)
                    pe.wait_ge(t_out, B * KT)
                    pe.matmul(PS[:, 0, 0:3], onesf[:], csum[:, 0:3], start=True, stop=True).then_inc(coef_ps, 1)
                    pe.wait_ge(coef_out, 1)
                    gate_up(0, 0, 0, 0, 0)
                    with pe.Fori(0, PAIRS - 1) as it:
                        pair(it, False)
                    pair(PAIRS - 1, True)


def lay_out(a):
    x = a["L0_attn_hidden_states"]
    xt = x.transpose(0, 2, 1).reshape(B, KT, P, S).transpose(0, 2, 1, 3)
    xn = x.reshape(B, QT, P, D).transpose(0, 2, 1, 3)
    wq = a["L0_attn_Wq"].reshape(QT, 8, HD, D).transpose(0, 2, 1, 3).reshape(NH * HD, D)
    wk = a["L0_attn_Wk"].reshape(NKV, HD, D).transpose(1, 0, 2).reshape(NKV * HD, D)
    w = np.concatenate([wq, wk, a["L0_attn_Wv"]], axis=0)
    wqkv = w.T.reshape(KT, P, -1).transpose(1, 0, 2)
    wo = a["L0_attn_Wo"].T.reshape(KT, P, D).transpose(1, 0, 2)

    def up(w):
        return w.reshape(NT, P, KT, P).transpose(0, 3, 2, 1).reshape(NT, P, D)

    def down(w):
        return w.T.reshape(NT, P, D)

    pairs = [(up, "w1"), (up, "w3"), (down, "w2")]
    wall = np.stack([np.stack([f(a[f"L0_ffn_{n}"]), f(a[f"L0_ffn_mean_{n}"])], axis=2) for f, n in pairs])
    return {"xt": xt, "x": xn, "wqkv": wqkv, "wo": wo, "wall": wall}


def constants():
    inv = (1.0 / 10000.0 ** (np.arange(0, HD, 2, dtype=np.float32) / HD)).astype(np.float32)
    ang = np.outer(np.arange(S, dtype=np.float32), inv).astype(np.float32)
    rows = np.repeat(ang.T, 8, axis=0)
    cos = np.concatenate([np.cos(rows), np.cos(rows)], axis=0)
    sin = np.concatenate([-np.sin(rows), np.sin(rows)], axis=0)
    return {"cos": cos.astype(np.float32), "sin": sin.astype(np.float32),
            "ident": np.eye(P, dtype=np.float32).astype(mybir.dt.np(BF16)), "identf": np.eye(P, dtype=np.float32),
            "mask": np.where(np.tri(P, dtype=bool), np.float32(0), np.float32(MASKED)).astype(mybir.dt.np(BF16))}


_ORDER = ("xt", "x", "wqkv", "wo", "wall", "cos", "sin", "ident", "identf", "mask")


def kernel(**inputs):
    from concourse import bacc
    from concourse.bass_utils import run_bass_kernel_spmd

    arrays = {**lay_out({k: np.asarray(v) for k, v in inputs.items()}), **constants()}
    arrays = {k: np.ascontiguousarray(arrays[k]) for k in _ORDER}
    nc = bacc.Bacc("TRN2", target_bir_lowering=False, num_devices=1)
    args = [nc.dram_tensor(k, a.shape, mybir.dt.from_np(a.dtype), kind="ExternalInput").ap() for k, a in arrays.items()]
    out = nc.dram_tensor("out", (B, P, QT, D), F32, kind="ExternalOutput").ap()
    layer(nc, *args, out)
    r = run_bass_kernel_spmd(nc, [arrays], core_ids=[0])
    return r.results[0]["out"].transpose(0, 2, 1, 3).reshape(B, S, D)
```

```python
from contextlib import ExitStack

import numpy as np
import concourse.bass as bass
from concourse import mybir

F32 = mybir.dt.float32
F32R = mybir.dt.float32r
BF16 = mybir.dt.bfloat16
ALU = mybir.AluOpType
ACT = mybir.ActivationFunctionType
AX_X = mybir.AxisListType.X

P = 128
B, S, D = 4, 512, 512
NH, NKV, HD = 32, 8, 16
GH = NH // NKV
F = 1792
KT = D // P
QT = S // P
NT = F // P
SCALE = float(HD) ** -0.5
EPS = 1e-5
MASKED = -3.0e38

ROWS = 6 * HD
Q_PARTS = (0, 0, 1, 1, 0, 2)
K_PARTS = (0, 1, 0, 1, 2, 0)

U1 = [(0, 0, 4), (1, 0, 2), (1, 2, 2)] + [(t, h, 1) for t in (2, 3) for h in range(GH)]
U2 = [(t, h, 1) for t in (0, 1) for h in range(GH)] + [(2, 0, 2), (2, 2, 2), (3, 0, 4)]
NU = len(U1)
LAST2 = [max(n for n, u in enumerate(U2) if u[0] == t) for t in range(QT)]
LAG = 2
NCO = NT

V_TILE, K_TILE = 5, 4
PROJECT = {0: (V_TILE, "cur"), 1: (2, "cur"), 2: (3, "cur"), 4: (0, "nxt"), 5: (K_TILE, "nxt"), 6: (1, "nxt")}
PROJECT_AT = (2, 4, 6, 8)
TURN = {1: 0, 3: 1}
ROPES = {1: 3, 2: 4, 4: 5, 5: 6, 6: 7}
SPLIT_X = {(2, 10): (0, 1), (3, 9): (2,), (3, 10): (3,)}
FIRST = ((K_TILE, 0), (0, 1), (1, 2))
N_ROPE = 5
OUT_STEP = 4


def uses(prev, cur, nxt):
    have, order = {"prev": prev, "cur": cur, "nxt": nxt}, []
    for st in range(NKV):
        if st == NKV - 1 and prev:
            order.append(("out", st))
        if cur if st else prev:
            order.append(("max", st))
        if st in PROJECT and have[PROJECT[st][1]]:
            order.append(("project", st))
        if st in TURN and cur:
            order.append(("turn", st))
        if OUT_STEP <= st < NKV - 1 and prev:
            order.append(("out", st))
    return {what: n for n, what in enumerate(order)}


class Section:

    def __init__(self, b, prev, cur, nxt):
        self.b, self.prev, self.cur, self.nxt = b, prev, cur, nxt
        self.uses = uses(prev, cur, nxt)
        first, full = len(uses(False, True, True)), len(uses(True, True, True))
        if prev and cur and nxt:
            self.g0, self.parity = b * full + (len(FIRST) + first - full), (len(FIRST) + first) % 2
        else:
            self.g0 = len(FIRST) + (first + 2 * full if prev else 0) + (0 if cur else len(uses(True, True, False)))
            self.parity = self.g0 % 2
        assert full % 2 == 0

    def has(self, who):
        return {"prev": self.prev, "cur": self.cur, "nxt": self.nxt}[who]

    def use(self, what, st):
        n = self.uses.get((what, st))
        return None if n is None else (self.g0 + n, (self.parity + n) % 2)

    def behind(self, st, lag):
        g = st - lag
        if g >= 0:
            return (self.b * NKV + g, g) if self.cur else None
        return (self.b * NKV + g, g + NKV) if self.prev else None

    def tile(self, st, lag):
        g = self.behind(st, lag)
        if g is None or g[1] % 2 == 0:
            return None
        d = st - lag
        j = (d - 1) // 2
        return (self.b * KT + j, j % KT, self.b + j // KT)


def split_tile(sec, st):
    k = {0: 0, 1: 1, 3: 2, 4: 3}.get(st)
    return None if k is None or not sec.prev else ((sec.b - 1) * KT + k, k)


class Run:

    def __init__(self, eng, section):
        self.eng, self.section = eng, section


BANK_P1, BANK_P2, BANK_O, BANK_G = 0, 2, 4, 6


def hold(eng, semaphore, value, passed):
    eng.wait_ge(semaphore, value)
    eng.sem_inc(passed, 1)


def layer(nc, xt, x, wqkv, wo, wall, cos, sin, ident, identf, mask, out):
    with ExitStack() as top:
        def sem(name):
            return top.enter_context(nc.semaphore(name))

        wq_in = [sem(f"wq_in{i}") for i in range(KT)]
        raw_in = sem("raw_in")
        xn_in = sem("xn_in")
        ready0 = sem("ready0")
        wsplit = sem("wsplit")
        xt_in = [sem(f"xt_in{i}") for i in range(2)]
        xhigh = sem("xhigh")
        xsplit = sem("xsplit")
        g_done = sem("g_done")
        g_free = sem("g_free")
        added = sem("added")
        hi_out = sem("hi_out")
        rest = sem("rest")
        mid_out = sem("mid_out")
        lo_out = sem("lo_out")
        q_in = [sem(f"q_in{i}") for i in range(4)]
        k_kept = sem("k_kept")
        k_in = [sem(f"k_in{i}") for i in range(2)]
        p1_done = sem("p1_done")
        p1_free = sem("p1_free")
        max_split = sem("max_split")
        max_in = sem("max_in")
        p2_done = sem("p2_done")
        exped = sem("exped")
        pv_done = sem("pv_done")
        o_out = sem("o_out")
        o_kept = sem("o_kept")
        o_in = [sem(f"o_in{i}") for i in range(4)]
        den_in = sem("den_in")
        den_inv = sem("den_inv")
        inv_kept = sem("inv_kept")
        inv_in = sem("inv_in")
        o_norm = sem("o_norm")
        o_high = sem("o_high")
        o_split = sem("o_split")
        co_in = [sem(f"co_in{i}") for i in range(2)]
        co_diff = sem("co_diff")
        co_abs = sem("co_abs")
        var_out = sem("var_out")
        std_out = sem("std_out")
        shift_out = sem("shift_out")
        x1_out = sem("x1_out")
        chain = sem("chain")
        coef_ps = sem("coef_ps")
        coef_out = sem("coef_out")
        t_done = sem("t_done")
        t_high = sem("t_high")
        t_out = sem("t_out")
        w_in = [sem(f"w_in{i}") for i in range(2)]
        w_diff = sem("w_diff")
        w_sign = sem("w_sign")
        w_out = sem("w_out")
        gu_done = sem("gu_done")
        sig_out = sem("sig_out")
        h_out = sem("h_out")
        y_done = sem("y_done")
        y_free = sem("y_free")
        fchain = sem("fchain")
        var2_out = sem("var2_out")
        std2_out = sem("std2_out")
        stored = sem("stored")
        passed = sem("passed")

        PS = top.enter_context(nc.psum_tensor("PS", [P, 8, 512], F32))
        y = top.enter_context(nc.sbuf_tensor("y", [P, B * QT, D], F32))
        idf = top.enter_context(nc.sbuf_tensor("idf", [P, P], F32))
        asum = top.enter_context(nc.sbuf_tensor("asum", [P, 3, NCO], F32))
        csum = top.enter_context(nc.sbuf_tensor("csum", [P, 4], F32))
        coef = top.enter_context(nc.sbuf_tensor("coef", [P, 4], F32))
        onesf = top.enter_context(nc.sbuf_tensor("onesf", [P, P], F32))
        eps = top.enter_context(nc.sbuf_tensor("eps", [P, 1], F32))
        bnst = top.enter_context(nc.sbuf_tensor("bnst", [P, QT, 6], F32))
        mv = top.enter_context(nc.sbuf_tensor("mv", [P, QT, 2], F32))
        sd = top.enter_context(nc.sbuf_tensor("sd", [P, QT], F32))
        mean = top.enter_context(nc.sbuf_tensor("mean", [P, QT], F32))
        shift = top.enter_context(nc.sbuf_tensor("shift", [P, QT], F32))
        rs = top.enter_context(nc.sbuf_tensor("rs", [P, QT], F32))

        o_dram = nc.dram_tensor("o_dram", (KT, 2 * GH, 2 * HD, S), F32, kind="Internal").ap()
        inv_dram = nc.dram_tensor("inv_dram", (KT, 2 * GH, S), F32, kind="Internal").ap()
        k_dram = nc.dram_tensor("k_dram", (3, HD, NKV, S), BF16, kind="Internal").ap()
        with ExitStack() as ctx:
            def sb(name, shape, dt):
                return ctx.enter_context(nc.sbuf_tensor(name, shape, dt))

            NC = NH * HD + 2 * NKV * HD
            NM = 3 * GH * QT
            wqH, wqL = sb("wqH", [P, KT, NC], F32R), sb("wqL", [P, KT, NC], F32R)
            woH, woL = sb("woH", [P, KT, D], F32R), sb("woL", [P, KT, D], F32R)
            Qs, Ks = sb("Qs", [P, NH, S], BF16), sb("Ks", [P, NKV, S], BF16)
            vT = sb("vT", [P, S], F32)
            V = sb("V", [P, QT, NKV, 2 * HD], F32)
            Pt = sb("Pt", [P, 2, GH, S], F32)
            xH, xL = sb("xH", [P, KT, S], F32R), sb("xL", [P, KT, S], F32R)
            xraw = sb("xraw", [P, 2, S], F32)
            cs, sn = sb("cs", [P, S], F32), sb("sn", [P, S], F32)
            idb, mk = sb("idb", [P, P], BF16), sb("mk", [P, P], BF16)
            rp = sb("rp", [P, 2, S], F32)
            parts = sb("parts", [P, 3, S], BF16)
            Oe = sb("Oe", [P, S], F32)
            Oc = sb("Oc", [P, KT, S], F32)
            den, inv = sb("den", [P, 2 * GH * S // P], F32), sb("inv", [P, 2 * GH * S // P], F32)
            Inv = sb("Inv", [P, S], F32)
            OH, OL = sb("OH", [P, KT, S], F32R), sb("OL", [P, KT, S], F32R)
            negM = sb("negM", [P, GH, QT], F32)
            negR = sb("negR", [P, GH, QT], F32)
            mp_all = sb("mp", [P, P], BF16)
            mp = mp_all[:, 0:NM].rearrange("p (a h t) -> p a h t", a=3, h=GH)
            mT = sb("mT", [NM, P], BF16)
            co = sb("co", [P, 2, 2, 512], F32)
            raw = Qs[:].rearrange("p h s -> p (h s)").bitcast(F32)
            Q0 = raw.shape[1] - KT * (NC + D)
            raw_q = raw[:, Q0:Q0 + KT * NC].rearrange("p (k n) -> p k n", k=KT)
            raw_o = raw[:, Q0 + KT * NC:].rearrange("p (k n) -> p k n", k=KT)

            def g_bank(parity):
                return PS[:, BANK_G + parity, :]

            def sections(run):
                run.section(Section(0, False, True, True))
                with run.eng.Fori(1, B - 1) as b:
                    run.section(Section(b, True, True, True))
                run.section(Section(B - 1, True, True, False))
                run.section(Section(B, True, False, False))

            with nc.Block() as block:

                @block.sync
                def _(sp):
                    for k in range(KT):
                        if k < 2:
                            sp.dma_start(xraw[:, k], xt[0, :, k, :]).then_inc(xt_in[k], 16)
                        sp.dma_start(raw_q[:, k], wqkv[:, k]).then_inc(wq_in[k], 16)
                    for k in range(2, KT):
                        sp.wait_ge(xsplit, k - 1)
                        sp.dma_start(xraw[:, k % 2, :], xt[0, :, k, :]).then_inc(xt_in[k % 2], 16)
                    for dst, src in ((cs[:], cos), (sn[:], sin), (idb[:], ident), (mk[:], mask), (idf[:], identf),
                                     (raw_o, wo)):
                        sp.dma_start(dst, src).then_inc(raw_in, 16)

                    def load_xt(b, k):
                        hold(sp, xsplit, b * KT + k - 1, passed)
                        sp.dma_start(xraw[:, k % 2, :], xt[b, :, k, :]).then_inc(xt_in[k % 2], 16)

                    def load_co(b, c):
                        hold(sp, co_abs, b * NCO + c + 1, passed)
                        sp.dma_start(co[:, c % 2], wall[b, c]).then_inc(co_in[c % 2], 16)

                    def stack_q(i, r, part, done):
                        hold(sp, done, r + 1, passed)
                        for n in range(6):
                            if Q_PARTS[n] == part:
                                sp.dma_start(Qs[HD * n:HD * (n + 1), 8 * i:8 * i + 8, :],
                                             parts[:, part, :]).then_inc(q_in[i], 16)

                    def keep_k(r, part, done):
                        hold(sp, done, r + 1, passed)
                        sp.dma_start(k_dram[part], parts[:, part, :]).then_inc(k_kept, 16)

                    def stack_k(b, half):
                        hold(sp, k_kept, b * 48 + 48, passed)
                        h = slice(4 * half, 4 * half + 4)
                        for n in range(6):
                            sp.dma_start(Ks[HD * n:HD * (n + 1), h, :], k_dram[K_PARTS[n], :, h, :]).then_inc(k_in[half], 16)

                    def stacks(tile, b, r, part):
                        done = (hi_out, mid_out, lo_out)[part]
                        if tile == K_TILE:
                            keep_k(r, part, done)
                            if part == 2:
                                stack_k(b, 0)
                        else:
                            stack_q(tile, r, part, done)

                    def section(sec):
                        b = sec.b
                        for st in range(NKV):
                            if sec.nxt and st < NCO // 2:
                                load_co(b, 2 * st)
                                load_co(b, 2 * st + 1)
                            if sec.nxt and st == 1:
                                load_xt(b + 1, 0)
                                load_xt(b + 1, 1)
                            if st == 2 and sec.cur:
                                if sec.prev:
                                    hold(sp, p2_done, b * NKV * NU, passed)
                                stack_k(b, 1)
                            ps = st - 1 if st else 7
                            r = ROPES.get(ps)
                            tile, who = PROJECT.get(ps, (None, "cur"))
                            mine = r is not None and sec.has(who)
                            if mine and ps in (4, 5, 6):
                                last = {4: 1, 5: 3, 6: 3}[ps]
                                hold(sp, p2_done, (b * NKV + last + 1) * NU, passed)
                            if mine and ps in (1, 2) and sec.prev:
                                last = {1: 5, 2: 7}[ps]
                                hold(sp, p2_done, (b * NKV + last + 1 - NKV) * NU, passed)
                            if mine:
                                stacks(tile, b + (who == "nxt"), r + b * N_ROPE, 0)
                            if sec.nxt and st == 3:
                                load_xt(b + 1, 2)
                                load_xt(b + 1, 3)
                            m = sec.use("max", st)
                            if m:
                                hold(sp, g_free, m[0] + 3, passed)
                                h = GH * sec.behind(st, 1)[1]
                                sp.dma_start(Qs[ROWS:ROWS + 3, h:h + GH, :], mT[:]).then_inc(max_in, 16)
                            t = sec.tile(st, 4)
                            if t:
                                hold(sp, den_inv, t[0] + 1, passed)
                                sp.dma_start(inv_dram[t[1]], inv[:]).then_inc(inv_kept, 16)
                            g = sec.behind(st, 3)
                            if g:
                                hold(sp, o_out, g[0] + 3, passed)
                                sp.dma_start(o_dram[g[1] // 2, GH * (g[1] % 2):GH * (g[1] % 2) + GH], Oe[:]
                                             ).then_inc(o_kept, 16)
                            if mine:
                                stacks(tile, b + (who == "nxt"), r + b * N_ROPE, 1)
                            t = sec.tile(st, 3)
                            if t:
                                hold(sp, o_kept, t[0] * 32 + 48, passed)
                                hold(sp, o_split, t[0] + 1, passed)
                                sp.dma_start(Oc[:, t[1], :], o_dram[t[1], :, 0:HD, :]).then_inc(o_in[t[1]], 16)
                                sp.dma_start(den[:], o_dram[t[1], :, HD, :].rearrange("h (c x) -> h c x", x=den.shape[1])
                                             ).then_inc(den_in, 16)
                            if mine:
                                stacks(tile, b + (who == "nxt"), r + b * N_ROPE, 2)
                            if not sec.prev and st >= NKV - B:
                                n = st - (NKV - B)
                                sp.dma_start(y[:, QT * n:QT * (n + 1), :], x[n]).then_inc(xn_in, 16)
                            t = sec.tile(st, 4)
                            if t:
                                hold(sp, o_norm, t[0] + 1, passed)
                                hold(sp, inv_kept, t[0] * 16 + 16, passed)
                                sp.dma_start(Inv[:], inv_dram[t[1]].unsqueeze(1).broadcast_to([2 * GH, HD, S])
                                             ).then_inc(inv_in, 16)

                    for tile, r in FIRST:
                        for part in range(3):
                            stacks(tile, 0, r, part)
                    sections(Run(sp, section))

                @block.gpsimd
                def _(pool):
                    def rope_add(r, n):
                        pool.wait_ge(g_free, n + 3)
                        pool.tensor_tensor(rp[:, 0], rp[:, 0], rp[:, 1], ALU.add).then_inc(added, 1)

                    def remainder(r):
                        pool.wait_ge(hi_out, r + 1)
                        pool.tensor_tensor(rp[:, 1], rp[:, 0], parts[:, 0], ALU.subtract).then_inc(rest, 1)

                    def low(r):
                        pool.wait_ge(mid_out, r + 1)
                        pool.tensor_tensor(parts[:, 2], rp[:, 1], parts[:, 1], ALU.subtract).then_inc(lo_out, 1)

                    def split_x(b, k):
                        pool.wait_ge(xhigh, b * KT + k + 1)
                        pool.tensor_tensor(xL[:, k], xraw[:, k % 2], xH[:, k].bitcast(F32), ALU.subtract
                                           ).then_inc(xsplit, 1)

                    def diff(b, c):
                        pool.wait_ge(co_in[c % 2], (b * (NCO // 2) + c // 2 + 1) * 16)
                        pool.tensor_tensor(co[:, c % 2, 0], co[:, c % 2, 0], co[:, c % 2, 1],
                                           ALU.subtract).then_inc(co_diff, 1)

                    def section(sec):
                        b = sec.b
                        for st in range(NKV):
                            ps = st - 1 if st else 7
                            mine = ps in ROPES and sec.has(PROJECT[ps][1])
                            r = ROPES.get(ps, 0) + b * N_ROPE
                            if mine:
                                rope_add(r, sec.use("project", ps)[0])
                            if mine:
                                remainder(r)
                            if sec.nxt and st < NCO // 2:
                                diff(b, 2 * st)
                            t = sec.tile(st, 5)
                            if t:
                                pool.wait_ge(o_in[t[1]], t[2] * 16 + 16)
                                pool.wait_ge(inv_in, t[0] * 16 + 16)
                                o = Oc[:, t[1], :]
                                pool.tensor_tensor(o, o, Inv[:], ALU.mult).then_inc(o_norm, 1)
                            if mine:
                                low(r)
                            if sec.nxt and st < NCO // 2:
                                diff(b, 2 * st + 1)
                            t = split_tile(sec, st)
                            if t:
                                pool.wait_ge(o_high, t[0] + 1)
                                pool.tensor_tensor(OL[:, t[1]], Oc[:, t[1]], OH[:, t[1]].bitcast(F32), ALU.subtract
                                                   ).then_inc(o_split, 1)
                            if sec.nxt and st in (2, 3):
                                split_x(b + 1, 2 * st - 4)
                                split_x(b + 1, 2 * st - 3)
                        if sec.prev:
                            pool.wait_ge(std_out, b)
                            pool.tensor_tensor(shift[:], mean[:], rs[:], ALU.mult).then_inc(shift_out, 1)

                    for k in range(KT):
                        split_x(0, k)
                    sections(Run(pool, section))

                @block.scalar
                def _(act):
                    def high(r):
                        act.wait_ge(added, r + 1)
                        act.activation(parts[:, 0], rp[:, 0], ACT.Copy).then_inc(hi_out, 1)

                    def middle(r):
                        act.wait_ge(rest, r + 1)
                        act.activation(parts[:, 1], rp[:, 1], ACT.Copy).then_inc(mid_out, 1)

                    def exp_unit(g, n):
                        t, h, m = U2[n]
                        w = S - P * t
                        act.wait_ge(p2_done, g[0] * NU + n + 1)
                        if h == 0:
                            act.wait_ge(pv_done, g[0] * QT + t + 1)
                        act.activation(Pt[:, t % 2, h:h + m, P * t:S],
                                       PS[:, BANK_P2 + (g[1] * NU + n) % 2, 0:m * w].rearrange("p (m w) -> p m w", m=m),
                                       ACT.Exp, scale=SCALE).then_inc(exped, 1)

                    def o_copy(g):
                        act.wait_ge(pv_done, g[0] * QT + QT + 2)
                        act.wait_ge(o_kept, g[0] * 16 + 16)
                        act.activation(Oe[:], PS[:, BANK_O + g[1] % 2, :], ACT.Copy).then_inc(o_out, 1)

                    def abs_sum(b, c):
                        act.wait_ge(co_diff, b * NCO + c + 1)
                        act.activation(co[:, c % 2, 1], co[:, c % 2, 0], ACT.Abs,
                                       accum_out=asum[:, b, c:c + 1]).then_inc(co_abs, 1)

                    def section(sec):
                        b = sec.b
                        for st in range(NKV):
                            ps = st - 1 if st else 7
                            mine = ps in ROPES and sec.has(PROJECT[ps][1])
                            r = ROPES.get(ps, 0) + b * N_ROPE
                            g = sec.behind(st, LAG)
                            for n in range(NU):
                                if g:
                                    exp_unit(g, n)
                                if n == 3 and mine:
                                    before = {1: (1, b + 1), 2: (2, b + 1), 4: (3, b + 1), 5: (0, b + 2),
                                              6: (K_TILE, b + 2)}[ps]
                                    if before[0] == K_TILE:
                                        act.wait_ge(k_kept, before[1] * 48)
                                    else:
                                        act.wait_ge(q_in[before[0]], before[1] * 96)
                                    high(r)
                                if n == 4 and sec.behind(st, 3):
                                    o_copy(sec.behind(st, 3))
                                if n == 7 and mine:
                                    middle(r)
                                if n in (8, 10) and sec.nxt and st < NCO // 2:
                                    abs_sum(b, 2 * st + (n == 10))
                                if n == 7 and st == 7 and sec.prev:
                                    act.wait_ge(var_out, b)
                                    act.activation(rs[:], sd[:], ACT.Sqrt).then_inc(std_out, 1)
                                if n == 6:
                                    t = split_tile(sec, st)
                                    if t:
                                        act.wait_ge(o_norm, t[0] + 2)
                                        act.activation(OH[:, t[1]], Oc[:, t[1]], ACT.Copy).then_inc(o_high, 1)

                        if sec.prev:
                            act.wait_ge(shift_out, b)
                            for t in (0, 1):
                                yt = y[:, (b - 1) * QT + t, :]
                                act.activation(yt, yt, ACT.Identity, bias=shift[:, t:t + 1], scale=rs[:, t:t + 1]
                                               ).then_inc(x1_out, 1)

                    for n, (tile, r) in enumerate(FIRST):
                        if n == 1:
                            act.wait_ge(k_kept, 48)
                        if n == 2:
                            act.wait_ge(q_in[0], 96)
                        high(r)
                        middle(r)
                    sections(Run(act, section))

                @block.vector
                def _(dve):
                    links = [0, 0]

                    def link(ins):
                        ins.then_inc(chain, 1)
                        links[1] += 1
                        return links[0] + links[1]

                    def high_x(b, k):
                        dve.wait_ge(xt_in[k % 2], (b * 2 + k // 2 + 1) * 16)
                        dve.tensor_copy(xH[:, k, :], xraw[:, k % 2, :]).then_inc(xhigh, 1)

                    def rope_products(r, use, i):
                        ps, half = g_bank(use[1]), P // 2
                        if i == 0:
                            dve.wait_ge(g_done, use[0] + 1)
                            if not isinstance(r, int) or r:
                                dve.wait_ge(lo_out, r)
                            dve.tensor_tensor(rp[:, 0], ps, cs[:], ALU.mult)
                        elif i == 1:
                            dve.tensor_tensor(rp[0:half, 1], ps[half:P, :], sn[0:half, :], ALU.mult)
                        else:
                            dve.tensor_tensor(rp[half:P, 1], ps[0:half, :], sn[half:P, :], ALU.mult).then_inc(g_free, 1)

                    def maxima(g, n):
                        t, h, m = U1[n]
                        w = P * (t + 1)
                        dve.wait_ge(p1_done, g[0] * NU + n + 1)
                        dve.tensor_reduce(negM[:, h:h + m, t],
                                          PS[:, BANK_P1 + (g[1] * NU + n) % 2, 0:m * w].rearrange("p (m w) -> p m w", m=m),
                                          AX_X, ALU.max, negate=True).then_inc(p1_free, 1)

                    def split_max(g):
                        dve.wait_ge(p1_free, g[0] * NU + NU + 2)
                        a = link(dve.tensor_copy(mp[:, 0], negM[:]))
                        dve.wait_ge(chain, a)
                        a = link(dve.tensor_tensor(negR[:], negM[:], mp[:, 0], ALU.subtract))
                        dve.wait_ge(chain, a)
                        a = link(dve.tensor_copy(mp[:, 1], negR[:]))
                        dve.wait_ge(chain, a)
                        dve.tensor_tensor(mp[:, 2], negR[:], mp[:, 1], ALU.subtract).then_inc(max_split, 1)

                    def max_copy(g, use):
                        dve.wait_ge(g_done, use[0] + 1)
                        dve.wait_ge(max_in, g[0] * 16 + 16)
                        dve.tensor_copy(mT[:], g_bank(use[1]).bitcast(BF16)[0:NM, 0:P]).then_inc(g_free, 1)

                    def turn_copy(half, use):
                        dve.wait_ge(g_done, use[0] + 1)
                        dve.tensor_copy(V[:, :, 4 * half:4 * half + 4, 0:HD],
                                        g_bank(use[1])[:, 0:2 * P].rearrange("p (t h d) -> p t h d", t=QT, d=HD)
                                        ).then_inc(g_free, 1)

                    def add_out(b, t, use):
                        yt = y[:, b * QT + t, :]
                        if t == 0:
                            dve.wait_ge(xn_in, B * 16)
                        dve.wait_ge(g_done, use[0] + 1)
                        dve.tensor_tensor(yt, g_bank(use[1]), yt, ALU.add).then_inc(g_free, 1)

                    def statistics(b, t, use):
                        yt = y[:, b * QT + t, :]
                        hold(dve, g_free, use[0] + 3, passed)
                        a = link(dve.bn_stats(bnst[:, t], yt))
                        hold(dve, chain, a, passed)
                        a = link(dve.bn_aggr(mv[:, t], bnst[:, t]))
                        if t == QT - 1:
                            dve.wait_ge(chain, a)
                            dve.tensor_scalar(mean[:], mv[:, :, 0], -1.0, None, ALU.mult)
                            a = link(dve.tensor_scalar(sd[:], mv[:, :, 1], EPS, None, ALU.add))
                            dve.wait_ge(chain, a)
                            dve.reciprocal(sd[:], sd[:]).then_inc(var_out, 1)

                    def first_tile(r, n):
                        for i in range(3):
                            rope_products(r, (n, n % 2), i)
                        dve.wait_ge(g_free, n + 3)
                        dve.tensor_tensor(rp[:, 0], rp[:, 0], rp[:, 1], ALU.add).then_inc(added, 1)
                        dve.wait_ge(hi_out, r + 1)
                        dve.tensor_tensor(rp[:, 1], rp[:, 0], parts[:, 0], ALU.subtract).then_inc(rest, 1)
                        dve.wait_ge(mid_out, r + 1)
                        dve.tensor_tensor(parts[:, 2], rp[:, 1], parts[:, 1], ALU.subtract).then_inc(lo_out, 1)

                    CH_SECTION = 3 * NKV + 2 * QT + 1
                    CH_FIRST = 2 * KT + 3 * NKV

                    def section(sec):
                        b = sec.b
                        full = sec.prev and sec.nxt
                        if full:
                            links[:] = [b * CH_SECTION + (CH_FIRST - CH_SECTION), 0]
                        elif sec.prev:
                            links[:] = [CH_FIRST + CH_SECTION * (b - 1), 0]
                        for st in range(NKV):
                            g = (b * NKV + st, st) if sec.cur else None
                            t = sec.tile(st, 4)
                            for n in range(NU):
                                if g:
                                    maxima(g, n)
                                if st and n == 0 and sec.use("project", st - 1) and st - 1 in ROPES:
                                    rope_products(ROPES[st - 1] + b * N_ROPE, sec.use("project", st - 1), 2)
                                if st and n == 1 and sec.use("turn", st - 1):
                                    turn_copy(TURN[st - 1], sec.use("turn", st - 1))
                                at = {1: (st - 1, 0), 2: (st - 1, 1)}
                                if st == NKV - 1:
                                    at[4], at[5] = (st, 0), (st, 1)
                                if n in at and sec.use("out", at[n][0]):
                                    of = at[n][0]
                                    (add_out, statistics)[at[n][1]](b - 1, of - OUT_STEP, sec.use("out", of))
                                if n == (4 if st == 7 else 3) and sec.use("max", st):
                                    max_copy(sec.behind(st, 1), sec.use("max", st))
                                if n == 4 and t:
                                    dve.wait_ge(den_in, t[0] * 16 + 16)
                                    dve.wait_ge(o_norm, t[0] + 1)
                                    dve.reciprocal(inv[:], den[:]).then_inc(den_inv, 1)
                                if not sec.prev and st == 1 and n in (2, 4, 6, 8):
                                    k = n // 2 - 1
                                    a = link(dve.tensor_copy(woH[:, k], raw_o[:, k]))
                                    dve.wait_ge(chain, a)
                                    dve.tensor_tensor(woL[:, k], raw_o[:, k], woH[:, k].bitcast(F32), ALU.subtract
                                                      ).then_inc(wsplit, 1)
                                if sec.nxt and (st, n) in SPLIT_X:
                                    for k in SPLIT_X[st, n]:
                                        high_x(b + 1, k)
                                use = sec.use("project", st)
                                if n in (9, 10) and use and st in ROPES:
                                    rope_products(ROPES[st] + b * N_ROPE, use, n - 9)
                                if n == 9 and use and st not in ROPES:
                                    dve.wait_ge(g_done, use[0] + 1)
                                    dve.tensor_copy(vT[:], g_bank(use[1])).then_inc(g_free, 1)
                            if g:
                                split_max(g)
                            if st == NKV - 1 and sec.prev:
                                dve.wait_ge(std_out, b)
                                for t in (2, 3):
                                    yt = y[:, (b - 1) * QT + t, :]
                                    dve.tensor_scalar(yt, yt, mv[:, t, 0:1], rs[:, t:t + 1], ALU.subtract,
                                                      ALU.mult).then_inc(x1_out, 1)
                        assert not full or links[1] == CH_SECTION

                    dve.memset(V[:], 1.0).then_inc(ready0, 1)
                    dve.memset(Ks[:], 1.0).then_inc(ready0, 1)
                    dve.memset(mp_all[:], 0.0).then_inc(ready0, 1)
                    dve.memset(eps[:], EPS).then_inc(ready0, 1)
                    dve.memset(onesf[:], 1.0).then_inc(ready0, 1)
                    for ring in (g_free, p1_free, exped, pv_done, o_out, co_abs):
                        dve.sem_inc(ring, 2)
                    for ring, free in ((o_norm, 1), (o_kept, 16), (max_in, 16), (o_split, 4)):
                        dve.sem_inc(ring, free)
                    for k in range(KT):
                        high_x(0, k)
                        dve.wait_ge(wq_in[k], 16)
                        a = link(dve.tensor_copy(wqH[:, k], raw_q[:, k]))
                        dve.wait_ge(chain, a)
                        dve.tensor_tensor(wqL[:, k], raw_q[:, k], wqH[:, k].bitcast(F32), ALU.subtract).then_inc(wsplit, 1)
                    dve.wait_ge(raw_in, 6 * 16)
                    dve.wait_ge(wsplit, KT)
                    for n, (_, r) in enumerate(FIRST):
                        first_tile(r, n)
                    sections(Run(dve, section))

                @block.tensor
                def _(pe):
                    def three(dst, stH, stL, moH, moL, k, n):
                        pe.matmul(dst, stH, moH, start=(k == 0), stop=False)
                        pe.matmul(dst, stH, moL, start=False, stop=False)
                        return pe.matmul(dst, stL, moH, start=False, stop=(k == n - 1))

                    def project(b, tile, use, k):
                        if k == 0:
                            pe.wait_ge(g_free, use[0] + 1)
                        pe.wait_ge(xsplit, b * KT + k + 1)
                        c = slice(P * tile, P * (tile + 1))
                        m = three(g_bank(use[1]), wqH[:, k, c], wqL[:, k, c], xH[:, k], xL[:, k], k, KT)
                        if k == KT - 1:
                            m.then_inc(g_done, 1)

                    def turn(half, use, v_use):
                        hold(pe, g_free, use[0] + 1, passed)
                        hold(pe, g_free, v_use + 3, passed)
                        rows = slice(64 * half, 64 * half + 64)
                        for t in range(QT):
                            m = pe.transpose(g_bank(use[1])[:, 64 * t:64 * (t + 1)], vT[rows, P * t:P * (t + 1)],
                                             idf[rows, rows])
                        m.then_inc(g_done, 1)

                    def pass1(g, n):
                        t, h0, m = U1[n]
                        w = P * (t + 1)
                        bank = PS[:, BANK_P1 + (g[1] * NU + n) % 2, :]
                        pe.wait_ge(p1_free, g[0] * NU + n + 1)
                        for i in range(m):
                            pe.matmul(bank[:, i * w:(i + 1) * w], Qs[0:ROWS, GH * g[1] + h0 + i, P * t:P * (t + 1)],
                                      Ks[0:ROWS, g[1], 0:w], start=True, stop=False)
                            last = pe.matmul(bank[:, (i + 1) * w - P:(i + 1) * w], idb[:], mk[:], start=False, stop=True)
                        last.then_inc(p1_done, 1)

                    def max_transpose(g, use):
                        pe.wait_ge(max_split, g[0] + 1)
                        pe.wait_ge(g_free, use[0] + 1)
                        pe.transpose(g_bank(use[1]).bitcast(BF16)[:, 0:P], mp_all[:], idb[:]).then_inc(g_done, 1)

                    def pass2(g, n):
                        t, h0, m = U2[n]
                        w = S - P * t
                        bank = PS[:, BANK_P2 + (g[1] * NU + n) % 2, :]
                        pe.wait_ge(exped, g[0] * NU + n + 1)
                        if n == 0:
                            pe.wait_ge(max_in, g[0] * 16 + 32)
                        for i in range(m):
                            pe.matmul(bank[:, i * w:(i + 1) * w], Ks[0:ROWS + 3, g[1], P * t:P * (t + 1)],
                                      Qs[0:ROWS + 3, GH * g[1] + h0 + i, P * t:S], start=True, stop=False)
                            last = pe.matmul(bank[:, i * w:i * w + P], mk[:], idb[:], start=False, stop=True)
                        last.then_inc(p2_done, 1)

                    def pv(g, t):
                        if t == 0:
                            pe.wait_ge(o_out, g[0] + 1)
                        pe.wait_ge(exped, g[0] * NU + LAST2[t] + 3)
                        for h in range(GH):
                            last = pe.matmul(PS[32 * h:32 * (h + 1), BANK_O + g[1] % 2, P * t:S], V[:, t, g[1], :],
                                             Pt[:, t % 2, h, P * t:S], start=(t == 0), stop=(t == QT - 1),
                                             tile_position=(0, 32 * h))
                        last.then_inc(pv_done, 1)

                    def project_out(b, t, use, k):
                        if k == 0:
                            pe.wait_ge(g_free, use[0] + 1)
                            if t == 0:
                                pe.wait_ge(wsplit, 2 * KT)
                        pe.wait_ge(o_split, b * KT + k + 5)
                        c = slice(P * t, P * (t + 1))
                        m = three(g_bank(use[1]), OH[:, k, c], OL[:, k, c], woH[:, k], woL[:, k], k, KT)
                        if k == KT - 1:
                            m.then_inc(g_done, 1)

                    def section(sec):
                        b = sec.b
                        for st in range(NKV):
                            if sec.cur:
                                if st % 2 == 0:
                                    pe.wait_ge(q_in[st // 2], (b + 1) * 96)
                                if st % 4 == 0:
                                    pe.wait_ge(k_in[st // 4], (b + 1) * 96)
                            g2, g3 = sec.behind(st, LAG), sec.behind(st, LAG + 1)
                            g1 = (b * NKV + st, st) if sec.cur else None
                            up, out_use = sec.use("project", st), sec.use("out", st)
                            for n in range(NU):
                                if g2:
                                    pass2(g2, n)
                                if g1:
                                    pass1(g1, n)
                                if n == 0 and g3:
                                    pv(g3, 2)
                                if n == 2 and g3:
                                    pv(g3, 3)
                                if n in PROJECT_AT and up:
                                    tile, who = PROJECT[st]
                                    project(b + (who == "nxt"), tile, up, PROJECT_AT.index(n))
                                if n == 6 and g2:
                                    pv(g2, 0)
                                if n == 9 and g2:
                                    pv(g2, 1)
                                if n == 9 and sec.use("turn", st):
                                    v_use = sec.use("project", 0)[0]
                                    turn(TURN[st], sec.use("turn", st), v_use)
                                if out_use:
                                    for k in ({1: (0,), 2: (1,), 3: (2, 3)} if st == 7 else {7: (0,), 9: (1,), 10: (2, 3)}
                                              ).get(n, ()):
                                        project_out(b - 1, st - OUT_STEP, out_use, k)
                                if n == 3 and sec.use("max", st):
                                    max_transpose(sec.behind(st, 1), sec.use("max", st))

                    pe.wait_ge(ready0, 5)
                    for k in range(KT):
                        pe.wait_ge(wsplit, k + 1)
                        for n in range(2):
                            project(0, FIRST[n][0], (n, n % 2), k)
                    for k in range(KT):
                        project(0, FIRST[2][0], (2, 0), k)
                    sections(Run(pe, section))

        with ExitStack() as ctx:
            def sb(name, shape, dt):
                return ctx.enter_context(nc.sbuf_tensor(name, shape, dt))

            XH, XL = sb("XH", [P, KT, B, S], F32R), sb("XL", [P, KT, B, S], F32R)
            Wr = sb("Wr", [P, 2, 3, 2, 512], F32)
            WH, WL = sb("WH", [P, 2, 3, 512], F32R), sb("WL", [P, 2, 3, 512], F32R)
            sg = sb("sg", [P, 2, S], F32)
            hb, hf = sb("hb", [P, S], F32), sb("hf", [P, S], F32)
            hH, hL = sb("hH", [P, 2, S], F32R), sb("hL", [P, 2, S], F32R)
            BANK_Y = 4
            PAIRS = NT // 2
            UNITS = 2 * B

            with nc.Block() as block:

                @block.sync
                def _(sp):
                    def load(i, par):
                        for t in range(3):
                            sp.dma_start(Wr[:, par, t], wall[t, i]).then_inc(w_in[par], 16)

                    load(0, 0)
                    load(1, 1)
                    with sp.Fori(0, PAIRS - 1) as it:
                        for par in range(2):
                            hold(sp, w_out, it * 6 + 3 * par + 3, passed)
                            load(it * 2 + par + 2, par)
                    for b in range(B):
                        for t in range(QT):
                            sp.wait_ge(x1_out, B * QT + b * QT + t + 1)
                            sp.dma_start(out[b, :, t, :], y[:, b * QT + t, :]).then_inc(stored, 16)
                    sp.wait_ge(stored, B * QT * 16)

                @block.gpsimd
                def _(pool):
                    def diff(it, par):
                        pool.wait_ge(w_in[par], (it + 1) * 48)
                        for t in range(3):
                            w = Wr[:, par, t]
                            pool.tensor_tensor(w[:, 0], w[:, 0], w[:, 1], ALU.subtract).then_inc(w_diff, 1)

                    diff(0, 0)
                    with pool.Fori(0, PAIRS - 1) as it:
                        diff(it, 1)
                        diff(it + 1, 0)
                    diff(PAIRS - 1, 1)

                @block.scalar
                def _(act):
                    def sign(n3, par, t):
                        act.wait_ge(w_diff, n3 + t + 1)
                        act.activation(Wr[:, par, t, 0], Wr[:, par, t, 0], ACT.Sign).then_inc(w_sign, 1)

                    def sigmoid(n, par):
                        act.wait_ge(gu_done, n * 2 + 1)
                        act.wait_ge(h_out, n + 1)
                        act.activation(sg[:, par], PS[:, 2 * par, :], ACT.Sigmoid).then_inc(sig_out, 1)

                    def std(b):
                        act.wait_ge(var2_out, b + 1)
                        act.activation(sd[:], mv[:, :, 1], ACT.Sqrt, bias=eps[:]).then_inc(std2_out, 1)

                    def pair(it, last):
                        for u in range(UNITS):
                            i, b = u // B, u % B
                            if not (last and u == UNITS - 1):
                                sigmoid(it * UNITS + u + 1, (u + 1) % 2)
                            if b < 3 and not (last and i == 1):
                                sign(it * 6 + 3 * i + 3, (i + 1) % 2, b)
                            if last and i == 1:
                                std(b)

                    for n in range(B * KT):
                        act.wait_ge(t_done, n + 1)
                        act.activation(XH[:, n % KT, n // KT, :], PS[:, n % 8, :], ACT.Copy).then_inc(t_high, 1)
                    for t in range(3):
                        sign(0, 0, t)
                    sigmoid(0, 0)
                    with act.Fori(0, PAIRS - 1) as it:
                        pair(it, False)
                    pair(PAIRS - 1, True)

                @block.vector
                def _(dve):
                    links = [0, 0]

                    def link(ins):
                        ins.then_inc(fchain, 1)
                        links[1] += 1
                        return links[0] + links[1]

                    def weights(n3, par, t):
                        dve.wait_ge(w_sign, n3 + t + 1)
                        w = Wr[:, par, t]
                        a = link(dve.scalar_tensor_tensor(out=w[:, 0], in0=w[:, 0], scalar=coef[:, t:t + 1],
                                                          in1=w[:, 1], op0=ALU.mult, op1=ALU.add))
                        dve.wait_ge(fchain, a)
                        a = link(dve.tensor_copy(WH[:, par, t], w[:, 0]))
                        dve.wait_ge(fchain, a)
                        dve.tensor_tensor(WL[:, par, t], w[:, 0], WH[:, par, t].bitcast(F32),
                                          ALU.subtract).then_inc(w_out, 1)

                    def silu(n, par):
                        dve.wait_ge(sig_out, n + 1)
                        a = link(dve.tensor_tensor(hb[:], PS[:, 2 * par, :], sg[:, par], ALU.mult))
                        dve.wait_ge(fchain, a)
                        dve.wait_ge(gu_done, n * 2 + 2)
                        a = link(dve.tensor_tensor(hf[:], PS[:, 2 * par + 1, :], hb[:], ALU.mult))
                        dve.wait_ge(fchain, a)
                        a = link(dve.tensor_copy(hH[:, par], hf[:]))
                        dve.wait_ge(fchain, a)
                        dve.tensor_tensor(hL[:, par], hf[:], hH[:, par].bitcast(F32), ALU.subtract).then_inc(h_out, 1)

                    def accumulate(n, b):
                        for t in range(QT):
                            yt = y[:, b * QT + t, :]
                            dve.wait_ge(y_done, n * QT + t + 1)
                            dve.wait_ge(y_free, n * QT + t + 1)
                            dve.tensor_tensor(yt, PS[:, BANK_Y + t, :], yt, ALU.add).then_inc(y_free, 1)

                    def norm(n, b):
                        for t in range(QT):
                            yt = y[:, b * QT + t, :]
                            dve.wait_ge(y_free, n * QT + t + 17)
                            a = link(dve.bn_stats(bnst[:, t], yt))
                            dve.wait_ge(fchain, a)
                            a = dve.bn_aggr(mv[:, t], bnst[:, t])
                        a.then_inc(var2_out, 1)
                        dve.wait_ge(std2_out, b + 1)
                        a = link(dve.reciprocal(rs[:], sd[:]))
                        dve.wait_ge(fchain, a)
                        for t in range(QT):
                            yt = y[:, b * QT + t, :]
                            dve.tensor_scalar(yt, yt, mv[:, t, 0:1], rs[:, t:t + 1], ALU.subtract,
                                              ALU.mult).then_inc(x1_out, 1)

                    def pair(it, last):
                        links[:] = [it * FCH_PAIR + FCH_START, 0]
                        for u in range(UNITS):
                            i, b, n = u // B, u % B, it * UNITS + u
                            if not (last and u == UNITS - 1):
                                silu(n + 1, (u + 1) % 2)
                            if b < 3 and not (last and i == 1):
                                weights(it * 6 + 3 * i + 3, (i + 1) % 2, b)
                            accumulate(n, b)
                            if last and i == 1:
                                norm(n, b)
                        if not last:
                            assert links[1] == FCH_PAIR

                    FCH_START = 1 + 2 * 3 + 3
                    FCH_PAIR = 3 * UNITS + 2 * 6

                    a = link(dve.tensor_reduce(csum[:, 0:3], asum[:], AX_X, ALU.add))
                    for ring, free in ((h_out, 2), (y_free, 16)):
                        dve.sem_inc(ring, free)
                    for n in range(B * KT):
                        dve.wait_ge(t_high, n + 1)
                        dve.tensor_tensor(XL[:, n % KT, n // KT, :], PS[:, n % 8, :],
                                          XH[:, n % KT, n // KT, :].bitcast(F32), ALU.subtract).then_inc(t_out, 1)
                    dve.wait_ge(coef_ps, 1)
                    dve.tensor_scalar(coef[:, 0:3], PS[:, 0, 0:3], 1.0 / (F * D), None, ALU.mult).then_inc(coef_out, 1)
                    dve.wait_ge(coef_out, 1)
                    for t in range(3):
                        weights(0, 0, t)
                    silu(0, 0)
                    assert links[1] == FCH_START
                    with dve.Fori(0, PAIRS - 1) as it:
                        pair(it, False)
                    pair(PAIRS - 1, True)

                @block.tensor
                def _(pe):
                    def three(dst, stH, stL, moH, moL, k, n):
                        pe.matmul(dst, stH, moH, start=(k == 0), stop=False)
                        pe.matmul(dst, stH, moL, start=False, stop=False)
                        return pe.matmul(dst, stL, moH, start=False, stop=(k == n - 1))

                    def gate_up(n, n3, par, wpar, b):
                        pe.wait_ge(h_out, n + 1)
                        for t in range(2):
                            pe.wait_ge(w_out, n3 + t + 1)
                            for k in range(KT):
                                c = slice(P * k, P * (k + 1))
                                m = three(PS[:, 2 * par + t, :], WH[:, wpar, t, c], WL[:, wpar, t, c],
                                          XH[:, k, b, :], XL[:, k, b, :], k, KT)
                            m.then_inc(gu_done, 1)

                    def down(n, n3, par, wpar):
                        pe.wait_ge(h_out, n + 3)
                        pe.wait_ge(w_out, n3 + 3)
                        for t in range(QT):
                            pe.wait_ge(y_free, n * QT + t + 13)
                            c = slice(P * t, P * (t + 1))
                            three(PS[:, BANK_Y + t, :], hH[:, par, c], hL[:, par, c], WH[:, wpar, 2], WL[:, wpar, 2],
                                  0, 1).then_inc(y_done, 1)

                    def pair(it, last):
                        for u in range(UNITS):
                            i, n, v = u // B, it * UNITS + u, u + 1
                            if v < UNITS:
                                gate_up(n + 1, it * 6 + 3 * (v // B), v % 2, v // B, v % B)
                            elif not last:
                                gate_up(n + 1, it * 6 + 6, 0, 0, 0)
                            down(n, it * 6 + 3 * i, u % 2, i)

                    for n in range(B * KT):
                        if n % KT == 0:
                            pe.wait_ge(x1_out, n + QT)
                        if n >= 8:
                            pe.wait_ge(t_out, n - 7)
                        k, b = n % KT, n // KT
                        for t in range(QT):
                            m = pe.transpose(PS[:, n % 8, P * t:P * (t + 1)], y[:, b * QT + t, P * k:P * (k + 1)], idf[:])
                        m.then_inc(t_done, 1)
                    pe.wait_ge(fchain, 1)
                    pe.wait_ge(t_out, B * KT)
                    pe.matmul(PS[:, 0, 0:3], onesf[:], csum[:, 0:3], start=True, stop=True).then_inc(coef_ps, 1)
                    pe.wait_ge(coef_out, 1)
                    gate_up(0, 0, 0, 0, 0)
                    with pe.Fori(0, PAIRS - 1) as it:
                        pair(it, False)
                    pair(PAIRS - 1, True)


def lay_out(a):
    x = a["L0_attn_hidden_states"]
    xt = x.transpose(0, 2, 1).reshape(B, KT, P, S).transpose(0, 2, 1, 3)
    xn = x.reshape(B, QT, P, D).transpose(0, 2, 1, 3)
    wq = a["L0_attn_Wq"].reshape(QT, 8, HD, D).transpose(0, 2, 1, 3).reshape(NH * HD, D)
    wk = a["L0_attn_Wk"].reshape(NKV, HD, D).transpose(1, 0, 2).reshape(NKV * HD, D)
    w = np.concatenate([wq, wk, a["L0_attn_Wv"]], axis=0)
    wqkv = w.T.reshape(KT, P, -1).transpose(1, 0, 2)
    wo = a["L0_attn_Wo"].T.reshape(KT, P, D).transpose(1, 0, 2)

    def up(w):
        return w.reshape(NT, P, KT, P).transpose(0, 3, 2, 1).reshape(NT, P, D)

    def down(w):
        return w.T.reshape(NT, P, D)

    pairs = [(up, "w1"), (up, "w3"), (down, "w2")]
    wall = np.stack([np.stack([f(a[f"L0_ffn_{n}"]), f(a[f"L0_ffn_mean_{n}"])], axis=2) for f, n in pairs])
    return {"xt": xt, "x": xn, "wqkv": wqkv, "wo": wo, "wall": wall}


def constants():
    inv = (1.0 / 10000.0 ** (np.arange(0, HD, 2, dtype=np.float32) / HD)).astype(np.float32)
    ang = np.outer(np.arange(S, dtype=np.float32), inv).astype(np.float32)
    rows = np.repeat(ang.T, 8, axis=0)
    cos = np.concatenate([np.cos(rows), np.cos(rows)], axis=0)
    sin = np.concatenate([-np.sin(rows), np.sin(rows)], axis=0)
    return {"cos": cos.astype(np.float32), "sin": sin.astype(np.float32),
            "ident": np.eye(P, dtype=np.float32).astype(mybir.dt.np(BF16)), "identf": np.eye(P, dtype=np.float32),
            "mask": np.where(np.tri(P, dtype=bool), np.float32(0), np.float32(MASKED)).astype(mybir.dt.np(BF16))}


_ORDER = ("xt", "x", "wqkv", "wo", "wall", "cos", "sin", "ident", "identf", "mask")


def kernel(**inputs):
    from concourse import bacc
    from concourse.bass_utils import run_bass_kernel_spmd

    arrays = {**lay_out({k: np.asarray(v) for k, v in inputs.items()}), **constants()}
    arrays = {k: np.ascontiguousarray(arrays[k]) for k in _ORDER}
    nc = bacc.Bacc("TRN2", target_bir_lowering=False, num_devices=1)
    args = [nc.dram_tensor(k, a.shape, mybir.dt.from_np(a.dtype), kind="ExternalInput").ap() for k, a in arrays.items()]
    out = nc.dram_tensor("out", (B, P, QT, D), F32, kind="ExternalOutput").ap()
    layer(nc, *args, out)
    r = run_bass_kernel_spmd(nc, [arrays], core_ids=[0])
    return r.results[0]["out"].transpose(0, 2, 1, 3).reshape(B, S, D)
```

```python
from contextlib import ExitStack

import numpy as np
import concourse.bass as bass
from concourse import mybir

F32 = mybir.dt.float32
F32R = mybir.dt.float32r
BF16 = mybir.dt.bfloat16
ALU = mybir.AluOpType
ACT = mybir.ActivationFunctionType
AX_X = mybir.AxisListType.X

P = 128
B, S, D = 4, 512, 512
NH, NKV, HD = 32, 8, 16
GH = NH // NKV
F = 1792
KT = D // P
QT = S // P
NT = F // P
SCALE = float(HD) ** -0.5
EPS = 1e-5
MASKED = -3.0e38

ROWS = 6 * HD
Q_PARTS = (0, 0, 1, 1, 0, 2)
K_PARTS = (0, 1, 0, 1, 2, 0)

U1 = [(0, 0, 4), (1, 0, 2), (1, 2, 2)] + [(t, h, 1) for t in (2, 3) for h in range(GH)]
U2 = [(t, h, 1) for t in (0, 1) for h in range(GH)] + [(2, 0, 2), (2, 2, 2), (3, 0, 4)]
NU = len(U1)
LAST2 = [max(n for n, u in enumerate(U2) if u[0] == t) for t in range(QT)]
LAG = 2
NCO = NT

V_TILE, K_TILE = 5, 4
PROJECT = {0: (V_TILE, "cur"), 1: (2, "cur"), 2: (3, "cur"), 4: (0, "nxt"), 5: (K_TILE, "nxt"), 6: (1, "nxt")}
PROJECT_AT = (3, 5, 7, 8)
TURN = {1: 0, 3: 1}
ROPES = {1: 3, 2: 4, 4: 5, 5: 6, 6: 7}
SPLIT_X = {(2, 10): (0, 1), (3, 9): (2,), (3, 10): (3,)}
FIRST = ((K_TILE, 0), (0, 1), (1, 2))
N_ROPE = 5
OUT_STEP = 4


def uses(prev, cur, nxt):
    have, order = {"prev": prev, "cur": cur, "nxt": nxt}, []
    for st in range(NKV):
        if st == NKV - 1 and prev:
            order.append(("out", st))
        if cur if st else prev:
            order.append(("max", st))
        if st in PROJECT and have[PROJECT[st][1]]:
            order.append(("project", st))
        if st in TURN and cur:
            order.append(("turn", st))
        if OUT_STEP <= st < NKV - 1 and prev:
            order.append(("out", st))
    return {what: n for n, what in enumerate(order)}


class Section:

    def __init__(self, b, prev, cur, nxt):
        self.b, self.prev, self.cur, self.nxt = b, prev, cur, nxt
        self.uses = uses(prev, cur, nxt)
        first, full = len(uses(False, True, True)), len(uses(True, True, True))
        if prev and cur and nxt:
            self.g0, self.parity = b * full + (len(FIRST) + first - full), (len(FIRST) + first) % 2
        else:
            self.g0 = len(FIRST) + (first + 2 * full if prev else 0) + (0 if cur else len(uses(True, True, False)))
            self.parity = self.g0 % 2
        assert full % 2 == 0

    def has(self, who):
        return {"prev": self.prev, "cur": self.cur, "nxt": self.nxt}[who]

    def use(self, what, st):
        n = self.uses.get((what, st))
        return None if n is None else (self.g0 + n, (self.parity + n) % 2)

    def behind(self, st, lag):
        g = st - lag
        if g >= 0:
            return (self.b * NKV + g, g) if self.cur else None
        return (self.b * NKV + g, g + NKV) if self.prev else None

    def tile(self, st, lag):
        g = self.behind(st, lag)
        if g is None or g[1] % 2 == 0:
            return None
        d = st - lag
        j = (d - 1) // 2
        return (self.b * KT + j, j % KT, self.b + j // KT)


def split_tile(sec, st):
    k = {0: 0, 1: 1, 3: 2, 4: 3}.get(st)
    return None if k is None or not sec.prev else ((sec.b - 1) * KT + k, k)


class Run:

    def __init__(self, eng, section):
        self.eng, self.section = eng, section


BANKS_P1, BANK_P2, BANK_O, BANK_G = (0, 1, 5), 2, 4, 6


def hold(eng, semaphore, value, passed):
    eng.wait_ge(semaphore, value)
    eng.sem_inc(passed, 1)


def layer(nc, xt, x, wqkv, wo, wall, cos, sin, ident, identf, mask, out):
    with ExitStack() as top:
        def sem(name):
            return top.enter_context(nc.semaphore(name))

        wq_in = [sem(f"wq_in{i}") for i in range(KT)]
        raw_in = sem("raw_in")
        xn_in = sem("xn_in")
        ready0 = sem("ready0")
        wsplit = sem("wsplit")
        xt_in = [sem(f"xt_in{i}") for i in range(2)]
        xhigh = sem("xhigh")
        xsplit = sem("xsplit")
        g_done = sem("g_done")
        g_free = sem("g_free")
        added = sem("added")
        hi_out = sem("hi_out")
        rest = sem("rest")
        mid_out = sem("mid_out")
        lo_out = sem("lo_out")
        q_in = [sem(f"q_in{i}") for i in range(4)]
        k_kept = sem("k_kept")
        k_in = [sem(f"k_in{i}") for i in range(2)]
        p1_done = sem("p1_done")
        p1_free = sem("p1_free")
        max_split = sem("max_split")
        max_in = sem("max_in")
        p2_done = sem("p2_done")
        exped = sem("exped")
        pv_done = sem("pv_done")
        o_out = sem("o_out")
        o_kept = sem("o_kept")
        o_in = [sem(f"o_in{i}") for i in range(4)]
        den_in = sem("den_in")
        den_inv = sem("den_inv")
        inv_kept = sem("inv_kept")
        inv_in = sem("inv_in")
        o_norm = sem("o_norm")
        o_high = sem("o_high")
        o_split = sem("o_split")
        co_in = [sem(f"co_in{i}") for i in range(2)]
        co_diff = sem("co_diff")
        co_abs = sem("co_abs")
        var_out = sem("var_out")
        std_out = sem("std_out")
        shift_out = sem("shift_out")
        x1_out = sem("x1_out")
        chain = sem("chain")
        coef_ps = sem("coef_ps")
        coef_out = sem("coef_out")
        t_done = sem("t_done")
        t_high = sem("t_high")
        t_out = sem("t_out")
        w_in = [sem(f"w_in{i}") for i in range(2)]
        w_diff = sem("w_diff")
        w_sign = sem("w_sign")
        w_out = sem("w_out")
        gu_done = sem("gu_done")
        sig_out = sem("sig_out")
        h_out = sem("h_out")
        y_done = sem("y_done")
        y_free = sem("y_free")
        fchain = sem("fchain")
        var2_out = sem("var2_out")
        std2_out = sem("std2_out")
        shift2_out = sem("shift2_out")
        normed = sem("normed")
        normed_late = sem("normed_late")
        stored = sem("stored")
        passed = sem("passed")

        PS = top.enter_context(nc.psum_tensor("PS", [P, 8, 512], F32))
        y = top.enter_context(nc.sbuf_tensor("y", [P, B * QT, D], F32))
        idf = top.enter_context(nc.sbuf_tensor("idf", [P, P], F32))
        asum = top.enter_context(nc.sbuf_tensor("asum", [P, 3, NCO], F32))
        csum = top.enter_context(nc.sbuf_tensor("csum", [P, 4], F32))
        coef = top.enter_context(nc.sbuf_tensor("coef", [P, 4], F32))
        onesf = top.enter_context(nc.sbuf_tensor("onesf", [P, P], F32))
        bnst = top.enter_context(nc.sbuf_tensor("bnst", [P, QT, 6], F32))
        mv = top.enter_context(nc.sbuf_tensor("mv", [P, QT, 2], F32))
        sd = top.enter_context(nc.sbuf_tensor("sd", [P, QT], F32))
        mean = top.enter_context(nc.sbuf_tensor("mean", [P, QT], F32))
        shift = top.enter_context(nc.sbuf_tensor("shift", [P, QT], F32))
        rs = top.enter_context(nc.sbuf_tensor("rs", [P, QT], F32))

        BANK_Y = 4
        PAIRS = NT // 2
        UNITS = 2 * B

        def turn_bank(n):
            return n % 2 + (2 if n >= (B - 1) * KT else 0)

        o_dram = nc.dram_tensor("o_dram", (KT, 2 * GH, 2 * HD, S), F32, kind="Internal").ap()
        inv_dram = nc.dram_tensor("inv_dram", (KT, 2 * GH, S), F32, kind="Internal").ap()
        k_dram = nc.dram_tensor("k_dram", (3, HD, NKV, S), BF16, kind="Internal").ap()
        with ExitStack() as ctx:
            def sb(name, shape, dt):
                return ctx.enter_context(nc.sbuf_tensor(name, shape, dt))

            NC = NH * HD + 2 * NKV * HD
            NM = 3 * GH * QT
            woH, woL = sb("woH", [P, KT, D], F32R), sb("woL", [P, KT, D], F32R)
            idb, mk = sb("idb", [P, P], BF16), sb("mk", [P, P], BF16)
            Oe = sb("Oe", [P, S], F32)
            Oc = sb("Oc", [P, KT, S], F32)
            den, inv = sb("den", [P, 2 * GH * S // P], F32), sb("inv", [P, 2 * GH * S // P], F32)
            Inv = sb("Inv", [P, S], F32)
            OH, OL = sb("OH", [P, KT, S], F32R), sb("OL", [P, KT, S], F32R)
            negM = sb("negM", [P, GH, QT], F32)
            negR = sb("negR", [P, GH, QT], F32)
            mp_all = sb("mp", [P, P], BF16)
            mp = mp_all[:, 0:NM].rearrange("p (a h t) -> p a h t", a=3, h=GH)
            mT = sb("mT", [NM, P], BF16)
            with ExitStack() as first:
                def sb1(name, shape, dt):
                    return first.enter_context(nc.sbuf_tensor(name, shape, dt))

                wqH, wqL = sb1("wqH", [P, KT, NC], F32R), sb1("wqL", [P, KT, NC], F32R)
                xH, xL = sb1("xH", [P, KT, S], F32R), sb1("xL", [P, KT, S], F32R)
                xraw = sb1("xraw", [P, 2, S], F32)
                cs, sn = sb1("cs", [P, S], F32), sb1("sn", [P, S], F32)
                vT = sb1("vT", [P, S], F32)
                rp = sb1("rp", [P, 2, S], F32)
                co = sb1("co", [P, 2, 2, 512], F32)
                parts = sb1("parts", [P, 3, S], BF16)
                Qs, Ks = sb1("Qs", [P, NH, S], BF16), sb1("Ks", [P, NKV, S], BF16)
                Pt = sb1("Pt", [P, 2, GH, S], F32)
                V = sb1("V", [P, QT, NKV, 2 * HD], F32)
            XH, XL = sb("XH", [P, KT, B, S], F32R), sb("XL", [P, KT, B, S], F32R)
            Wr, WH, WL = [], [], []
            for i in range(2):
                Wr.append(sb(f"Wr{i}", [P, 3, 2, 512], F32))
                WH.append(sb(f"WH{i}", [P, 3, 512], F32R))
                WL.append(sb(f"WL{i}", [P, 3, 512], F32R))
            sg = sb("sg", [P, 2, S], F32)
            hH, hL = sb("hH", [P, 2, S], F32R), sb("hL", [P, 2, S], F32R)
            hb, hf = sb("hb", [P, S], F32), sb("hf", [P, S], F32)
            raw = Qs[:].rearrange("p h s -> p (h s)").bitcast(F32)
            Q0 = NH * S // 2 - KT * (NC + D)
            raw_q = raw[:, Q0:Q0 + KT * NC].rearrange("p (k n) -> p k n", k=KT)
            raw_o = raw[:, Q0 + KT * NC:].rearrange("p (k n) -> p k n", k=KT)

            def g_bank(parity):
                return PS[:, BANK_G + parity, :]

            def sections(run):
                run.section(Section(0, False, True, True))
                with run.eng.Fori(1, B - 1) as b:
                    run.section(Section(b, True, True, True))
                run.section(Section(B - 1, True, True, False))
                run.section(Section(B, True, False, False))

            with nc.Block() as block:

                @block.sync
                def _(sp):
                    for k in range(KT):
                        if k < 2:
                            sp.dma_start(xraw[:, k], xt[0, :, k, :]).then_inc(xt_in[k], 16)
                        sp.dma_start(raw_q[:, k], wqkv[:, k]).then_inc(wq_in[k], 16)
                    for k in range(2, KT):
                        sp.wait_ge(xsplit, k - 1)
                        sp.dma_start(xraw[:, k % 2, :], xt[0, :, k, :]).then_inc(xt_in[k % 2], 16)
                    for dst, src in ((cs[:], cos), (sn[:], sin), (idb[:], ident), (mk[:], mask), (idf[:], identf),
                                     (raw_o, wo)):
                        sp.dma_start(dst, src).then_inc(raw_in, 16)

                    def load(i, par):
                        for t in range(3):
                            sp.dma_start(Wr[par][:, t], wall[t, i]).then_inc(w_in[par], 16)

                    def load_xt(b, k):
                        hold(sp, xsplit, b * KT + k - 1, passed)
                        sp.dma_start(xraw[:, k % 2, :], xt[b, :, k, :]).then_inc(xt_in[k % 2], 16)

                    def load_co(b, c):
                        hold(sp, co_abs, b * NCO + c + 1, passed)
                        sp.dma_start(co[:, c % 2], wall[b, c]).then_inc(co_in[c % 2], 16)

                    def stack_q(i, r, part, done):
                        hold(sp, done, r + 1, passed)
                        for n in range(6):
                            if Q_PARTS[n] == part:
                                sp.dma_start(Qs[HD * n:HD * (n + 1), 8 * i:8 * i + 8, :],
                                             parts[:, part, :]).then_inc(q_in[i], 16)

                    def keep_k(r, part, done):
                        hold(sp, done, r + 1, passed)
                        sp.dma_start(k_dram[part], parts[:, part, :]).then_inc(k_kept, 16)

                    def stack_k(b, half):
                        hold(sp, k_kept, b * 48, passed)
                        h = slice(4 * half, 4 * half + 4)
                        for n in range(6):
                            sp.dma_start(Ks[HD * n:HD * (n + 1), h, :], k_dram[K_PARTS[n], :, h, :]).then_inc(k_in[half], 16)

                    def stacks(tile, b, r, part):
                        done = (hi_out, mid_out, lo_out)[part]
                        if tile == K_TILE and isinstance(r, int) and r == 0:
                            sp.wait_ge(done, 1)
                            for n in range(6):
                                if K_PARTS[n] == part:
                                    sp.dma_start(Ks[HD * n:HD * (n + 1), :, :], parts[:, part, :]).then_inc(k_in[0], 16)
                        elif tile == K_TILE:
                            keep_k(r, part, done)
                            if part == 2:
                                stack_k(b, 0)
                        else:
                            stack_q(tile, r, part, done)

                    def section(sec):
                        b = sec.b
                        for st in range(NKV):
                            if not sec.cur and st == 0:
                                sp.wait_ge(p2_done, (B * NKV - 2) * NU)
                                load(0, 0)
                            if sec.nxt and st < NCO // 2:
                                load_co(b, 2 * st)
                                load_co(b, 2 * st + 1)
                            if sec.nxt and st == 1:
                                load_xt(b + 1, 0)
                                load_xt(b + 1, 1)
                            if st == 2 and sec.cur and sec.prev:
                                hold(sp, p2_done, b * NKV * NU, passed)
                                stack_k(b, 1)
                            ps = st - 1 if st else 7
                            r = ROPES.get(ps)
                            tile, who = PROJECT.get(ps, (None, "cur"))
                            mine = r is not None and sec.has(who)
                            if mine and ps in (4, 5, 6):
                                last = {4: 1, 5: 3, 6: 3}[ps]
                                hold(sp, p2_done, (b * NKV + last + 1) * NU, passed)
                            if mine and ps in (1, 2) and sec.prev:
                                last = {1: 5, 2: 7}[ps]
                                hold(sp, p2_done, (b * NKV + last + 1 - NKV) * NU, passed)
                            if mine:
                                stacks(tile, b + (who == "nxt"), r + b * N_ROPE, 0)
                            if sec.nxt and st == 3:
                                load_xt(b + 1, 2)
                                load_xt(b + 1, 3)
                            m = sec.use("max", st)
                            if m:
                                hold(sp, g_free, m[0] + 3, passed)
                                h = GH * sec.behind(st, 1)[1]
                                sp.dma_start(Qs[ROWS:ROWS + 3, h:h + GH, :], mT[:]).then_inc(max_in, 16)
                            t = sec.tile(st, 4)
                            if t:
                                hold(sp, den_inv, t[0] + 1, passed)
                                sp.dma_start(inv_dram[t[1]], inv[:]).then_inc(inv_kept, 16)
                            g = sec.behind(st, 3)
                            if g:
                                hold(sp, o_out, g[0] + 2, passed)
                                sp.dma_start(o_dram[g[1] // 2, GH * (g[1] % 2):GH * (g[1] % 2) + GH], Oe[:]
                                             ).then_inc(o_kept, 16)
                            if mine:
                                stacks(tile, b + (who == "nxt"), r + b * N_ROPE, 1)
                            t = sec.tile(st, 3)
                            if t:
                                hold(sp, o_kept, t[0] * 32 + 48, passed)
                                hold(sp, o_split, t[0] + 1, passed)
                                sp.dma_start(Oc[:, t[1], :], o_dram[t[1], :, 0:HD, :]).then_inc(o_in[t[1]], 16)
                                sp.dma_start(den[:], o_dram[t[1], :, HD, :].rearrange("h (c x) -> h c x", x=den.shape[1])
                                             ).then_inc(den_in, 16)
                            if mine:
                                stacks(tile, b + (who == "nxt"), r + b * N_ROPE, 2)
                            if not sec.prev and st >= NKV - B:
                                n = st - (NKV - B)
                                sp.dma_start(y[:, QT * n:QT * (n + 1), :], x[n]).then_inc(xn_in, 16)
                            t = sec.tile(st, 4)
                            if t:
                                hold(sp, o_norm, t[0] + 1, passed)
                                hold(sp, inv_kept, t[0] * 16 + 16, passed)
                                sp.dma_start(Inv[:], inv_dram[t[1]].unsqueeze(1).broadcast_to([2 * GH, HD, S])
                                             ).then_inc(inv_in, 16)
                            if not sec.cur and st == 4:
                                load(1, 1)

                    for tile, r in FIRST:
                        for part in range(3):
                            stacks(tile, 0, r, part)
                    sections(Run(sp, section))
                    with sp.Fori(0, PAIRS - 1) as it:
                        for par in range(2):
                            hold(sp, w_out, it * 6 + 3 * par + 3, passed)
                            load(it * 2 + par + 2, par)
                    for b in range(B - 1):
                        sp.wait_ge(normed, (b + 1) * QT)
                        sp.dma_start(out[b], y[:, b * QT:(b + 1) * QT, :]).then_inc(stored, 16)
                    for n in range(2):
                        for done, count, t in ((normed, (B - 1) * QT, n), (normed_late, 0, n + 2)):
                            sp.wait_ge(done, count + n + 1)
                            sp.dma_start(out[B - 1, :, t, :], y[:, (B - 1) * QT + t, :]).then_inc(stored, 16)
                    sp.wait_ge(stored, (B - 1 + QT) * 16)

                @block.gpsimd
                def _(pool):
                    def weight_diff(it, par):
                        pool.wait_ge(w_in[par], (it + 1) * 48)
                        for t in range(3):
                            w = Wr[par][:, t]
                            pool.tensor_tensor(w[:, 0], w[:, 0], w[:, 1], ALU.subtract).then_inc(w_diff, 1)

                    def rope_add(r, n):
                        pool.wait_ge(g_free, n + 3)
                        pool.tensor_tensor(rp[:, 0], rp[:, 0], rp[:, 1], ALU.add).then_inc(added, 1)

                    def remainder(r):
                        pool.wait_ge(hi_out, r + 1)
                        pool.tensor_tensor(rp[:, 1], rp[:, 0], parts[:, 0], ALU.subtract).then_inc(rest, 1)

                    def low(r):
                        pool.wait_ge(mid_out, r + 1)
                        pool.tensor_tensor(parts[:, 2], rp[:, 1], parts[:, 1], ALU.subtract).then_inc(lo_out, 1)

                    def split_x(b, k):
                        pool.wait_ge(xhigh, b * KT + k + 1)
                        pool.tensor_tensor(xL[:, k], xraw[:, k % 2], xH[:, k].bitcast(F32), ALU.subtract
                                           ).then_inc(xsplit, 1)

                    def diff(b, c):
                        pool.wait_ge(co_in[c % 2], (b * (NCO // 2) + c // 2 + 1) * 16)
                        pool.tensor_tensor(co[:, c % 2, 0], co[:, c % 2, 0], co[:, c % 2, 1],
                                           ALU.subtract).then_inc(co_diff, 1)

                    def section(sec):
                        b = sec.b
                        for st in range(NKV):
                            ps = st - 1 if st else 7
                            mine = ps in ROPES and sec.has(PROJECT[ps][1])
                            r = ROPES.get(ps, 0) + b * N_ROPE
                            if mine:
                                rope_add(r, sec.use("project", ps)[0])
                            if mine:
                                remainder(r)
                            if sec.nxt and st < NCO // 2:
                                diff(b, 2 * st)
                            t = sec.tile(st, 5)
                            if t:
                                pool.wait_ge(o_in[t[1]], t[2] * 16 + 16)
                                pool.wait_ge(inv_in, t[0] * 16 + 16)
                                o = Oc[:, t[1], :]
                                pool.tensor_tensor(o, o, Inv[:], ALU.mult).then_inc(o_norm, 1)
                            if mine:
                                low(r)
                            if sec.nxt and st < NCO // 2:
                                diff(b, 2 * st + 1)
                            t = split_tile(sec, st)
                            if t:
                                pool.wait_ge(o_high, t[0] + 1)
                                pool.tensor_tensor(OL[:, t[1]], Oc[:, t[1]], OH[:, t[1]].bitcast(F32), ALU.subtract
                                                   ).then_inc(o_split, 1)
                            if sec.nxt and st in (2, 3):
                                split_x(b + 1, 2 * st - 4)
                                split_x(b + 1, 2 * st - 3)
                            if not sec.cur and st in (0, 4):
                                weight_diff(0, st // 4)
                        if sec.prev:
                            pool.wait_ge(std_out, b)
                            pool.tensor_tensor(shift[:], mean[:], rs[:], ALU.mult).then_inc(shift_out, 1)

                    for k in range(KT):
                        split_x(0, k)
                    sections(Run(pool, section))
                    with pool.Fori(1, PAIRS) as it:
                        weight_diff(it, 0)
                        weight_diff(it, 1)
                    for b in range(B):
                        pool.wait_ge(std2_out, b + 1)
                        pool.tensor_tensor(shift[:], mean[:], rs[:], ALU.mult).then_inc(shift2_out, 1)

                @block.scalar
                def _(act):
                    def sign(n3, par, t):
                        act.wait_ge(w_diff, n3 + t + 1)
                        act.activation(Wr[par][:, t, 0], Wr[par][:, t, 0], ACT.Sign).then_inc(w_sign, 1)

                    def sigmoid(n, par):
                        act.wait_ge(gu_done, n * 2 + 1)
                        act.wait_ge(h_out, n + 1)
                        act.activation(sg[:, par], PS[:, 2 * par, :], ACT.Sigmoid).then_inc(sig_out, 1)

                    def std(b):
                        act.wait_ge(var2_out, b + 1)
                        act.activation(rs[:], sd[:], ACT.Sqrt).then_inc(std2_out, 1)
                        act.wait_ge(shift2_out, b + 1)
                        for t in range(QT if b < B - 1 else 2):
                            yt = y[:, b * QT + t, :]
                            act.activation(yt, yt, ACT.Identity, bias=shift[:, t:t + 1], scale=rs[:, t:t + 1]
                                           ).then_inc(normed, 1)

                    def pair(it, first, last):
                        for u in range(UNITS):
                            i, b = u // B, u % B
                            if first and u == 2:
                                for n in range((B - 1) * KT, B * KT):
                                    turned_high(n)
                            if not (last and u == UNITS - 1) and not (first and u == 0):
                                sigmoid(it * UNITS + u + 1, (u + 1) % 2)
                            if b < 3 and not (last and i == 1) and not (first and i == 0):
                                sign(it * 6 + 3 * i + 3, (i + 1) % 2, b)
                            if last and i == 1:
                                for done in {0: (), B - 1: (B - 2, B - 1)}.get(b, (b - 1,)):
                                    std(done)

                    def turned_high(n):
                        act.wait_ge(t_done, n + 1)
                        act.activation(XH[:, n % KT, n // KT, :], PS[:, turn_bank(n), :], ACT.Copy).then_inc(t_high, 1)

                    def begin_ffn():
                        sigmoid(0, 0)
                        sigmoid(1, 1)

                    def high(r):
                        act.wait_ge(added, r + 1)
                        act.activation(parts[:, 0], rp[:, 0], ACT.Copy).then_inc(hi_out, 1)

                    def middle(r):
                        act.wait_ge(rest, r + 1)
                        act.activation(parts[:, 1], rp[:, 1], ACT.Copy).then_inc(mid_out, 1)

                    def exp_unit(g, n):
                        t, h, m = U2[n]
                        w = S - P * t
                        act.wait_ge(p2_done, g[0] * NU + n + 1)
                        if h == 0:
                            act.wait_ge(pv_done, g[0] * QT + t + 1)
                        act.activation(Pt[:, t % 2, h:h + m, P * t:S],
                                       PS[:, BANK_P2 + (g[1] * NU + n) % 2, 0:m * w].rearrange("p (m w) -> p m w", m=m),
                                       ACT.Exp, scale=SCALE).then_inc(exped, 1)

                    def o_copy(g):
                        act.wait_ge(pv_done, g[0] * QT + QT + 2)
                        act.wait_ge(o_kept, g[0] * 16 + 16)
                        act.activation(Oe[:], PS[:, BANK_O, :], ACT.Copy).then_inc(o_out, 1)

                    def abs_sum(b, c):
                        act.wait_ge(co_diff, b * NCO + c + 1)
                        act.activation(co[:, c % 2, 1], co[:, c % 2, 0], ACT.Abs,
                                       accum_out=asum[:, b, c:c + 1]).then_inc(co_abs, 1)

                    def section(sec):
                        b = sec.b
                        for st in range(NKV):
                            ps = st - 1 if st else 7
                            mine = ps in ROPES and sec.has(PROJECT[ps][1])
                            r = ROPES.get(ps, 0) + b * N_ROPE
                            g = sec.behind(st, LAG)
                            for n in range(NU):
                                if g:
                                    exp_unit(g, n)
                                if n == 3 and mine:
                                    before = {1: (1, b + 1), 2: (2, b + 1), 4: (3, b + 1), 5: (0, b + 2),
                                              6: (K_TILE, b + 2)}[ps]
                                    if before[0] == K_TILE:
                                        act.wait_ge(k_kept, before[1] * 48 - 48)
                                    else:
                                        act.wait_ge(q_in[before[0]], before[1] * 96)
                                    high(r)
                                if n == 4 and sec.behind(st, 3):
                                    o_copy(sec.behind(st, 3))
                                if n == 7 and mine:
                                    middle(r)
                                if n in (8, 10) and sec.nxt and st < NCO // 2:
                                    abs_sum(b, 2 * st + (n == 10))
                                if n == 7 and st == 7 and sec.prev:
                                    act.wait_ge(var_out, b)
                                    act.activation(rs[:], sd[:], ACT.Sqrt).then_inc(std_out, 1)
                                if not sec.cur and st < 2 and n in (2, 4, 6, 8):
                                    turned_high(4 * st + n // 2 - 1)
                                if not sec.cur and st == 1 and n >= 8:
                                    sign(0, 0, n - 8)
                                if n == 6:
                                    t = split_tile(sec, st)
                                    if t:
                                        act.wait_ge(o_norm, t[0] + 2)
                                        act.activation(OH[:, t[1]], Oc[:, t[1]], ACT.Copy).then_inc(o_high, 1)

                            if not sec.cur and st == 2:
                                for n in range(2 * KT, 3 * KT):
                                    turned_high(n)
                            if not sec.cur and st == 3:
                                begin_ffn()
                            if not sec.cur and st == 4:
                                for t in range(3):
                                    sign(3, 1, t)
                        if sec.prev:
                            act.wait_ge(shift_out, b)
                            for t in (0, 1):
                                yt = y[:, (b - 1) * QT + t, :]
                                act.activation(yt, yt, ACT.Identity, bias=shift[:, t:t + 1], scale=rs[:, t:t + 1]
                                               ).then_inc(x1_out, 1)

                    for n, (tile, r) in enumerate(FIRST):
                        if n == 1:
                            act.wait_ge(k_in[0], 96)
                        if n == 2:
                            act.wait_ge(q_in[0], 96)
                        high(r)
                        middle(r)
                    sections(Run(act, section))
                    pair(0, True, False)
                    with act.Fori(1, PAIRS - 1) as it:
                        pair(it, False, False)
                    pair(PAIRS - 1, False, True)

                @block.vector
                def _(dve):
                    flinks = [0, 0]

                    def flink(ins):
                        ins.then_inc(fchain, 1)
                        flinks[1] += 1
                        return flinks[0] + flinks[1]

                    def weights(n3, par, t):
                        dve.wait_ge(w_sign, n3 + t + 1)
                        w = Wr[par][:, t]
                        a = flink(dve.scalar_tensor_tensor(out=w[:, 0], in0=w[:, 0], scalar=coef[:, t:t + 1],
                                                          in1=w[:, 1], op0=ALU.mult, op1=ALU.add))
                        dve.wait_ge(fchain, a)
                        a = flink(dve.tensor_copy(WH[par][:, t], w[:, 0]))
                        dve.wait_ge(fchain, a)
                        dve.tensor_tensor(WL[par][:, t], w[:, 0], WH[par][:, t].bitcast(F32),
                                          ALU.subtract).then_inc(w_out, 1)

                    def silu(n, par):
                        dve.wait_ge(sig_out, n + 1)
                        a = flink(dve.tensor_tensor(hb[:], PS[:, 2 * par, :], sg[:, par], ALU.mult))
                        dve.wait_ge(fchain, a)
                        dve.wait_ge(gu_done, n * 2 + 2)
                        a = flink(dve.tensor_tensor(hf[:], PS[:, 2 * par + 1, :], hb[:], ALU.mult))
                        dve.wait_ge(fchain, a)
                        a = flink(dve.tensor_copy(hH[:, par], hf[:]))
                        dve.wait_ge(fchain, a)
                        dve.tensor_tensor(hL[:, par], hf[:], hH[:, par].bitcast(F32), ALU.subtract).then_inc(h_out, 1)

                    def accumulate(n, b):
                        for t in range(QT):
                            yt = y[:, b * QT + t, :]
                            dve.wait_ge(y_done, n * QT + t + 1)
                            dve.wait_ge(y_free, n * QT + t + 1)
                            dve.tensor_tensor(yt, PS[:, BANK_Y + t, :], yt, ALU.add).then_inc(y_free, 1)

                    def norm(n, b):
                        for t in range(QT):
                            yt = y[:, b * QT + t, :]
                            dve.wait_ge(y_free, n * QT + t + 17)
                            a = flink(dve.bn_stats(bnst[:, t], yt))
                            dve.wait_ge(fchain, a)
                            a = flink(dve.bn_aggr(mv[:, t], bnst[:, t]))
                        dve.wait_ge(fchain, a)
                        if b:
                            dve.wait_ge(normed, b * QT)
                        dve.tensor_scalar(mean[:], mv[:, :, 0], -1.0, None, ALU.mult)
                        a = flink(dve.tensor_scalar(sd[:], mv[:, :, 1], EPS, None, ALU.add))
                        dve.wait_ge(fchain, a)
                        dve.reciprocal(sd[:], sd[:]).then_inc(var2_out, 1)
                        if b == B - 1:
                            dve.wait_ge(std2_out, b + 1)
                            for t in (2, 3):
                                yt = y[:, b * QT + t, :]
                                dve.tensor_scalar(yt, yt, mv[:, t, 0:1], rs[:, t:t + 1], ALU.subtract,
                                                  ALU.mult).then_inc(normed_late, 1)

                    def pair(it, first, last):
                        if not first:
                            flinks[:] = [(it - 1) * FCH_PAIR + FCH_START, 0]
                        for u in range(UNITS):
                            i, b, n = u // B, u % B, it * UNITS + u
                            if first and u == 2:
                                for m in range((B - 1) * KT, B * KT):
                                    turned_low(m)
                            if not (last and u == UNITS - 1) and not (first and u == 0):
                                silu(n + 1, (u + 1) % 2)
                            if first and u == 0:
                                weights(3, 1, 2)
                            elif b < 3 and not (last and i == 1) and not (first and i == 0):
                                weights(it * 6 + 3 * i + 3, (i + 1) % 2, b)
                            accumulate(n, b)
                            if last and i == 1:
                                norm(n, b)
                        assert first or last or flinks[1] == FCH_PAIR
                        assert not first or flinks[1] == FCH_START

                    FCH_PAIR = 3 * UNITS + 2 * 6
                    FCH_START = 1 + 2 * 3 + 3 + FCH_PAIR

                    def turned_low(n):
                        dve.wait_ge(t_high, n + 1)
                        dve.tensor_tensor(XL[:, n % KT, n // KT, :], PS[:, turn_bank(n), :],
                                          XH[:, n % KT, n // KT, :].bitcast(F32), ALU.subtract).then_inc(t_out, 1)

                    def coefficients():
                        dve.wait_ge(co_abs, 3 * NCO + 2)
                        flink(dve.tensor_reduce(csum[:, 0:3], asum[:], AX_X, ALU.add))

                    def means():
                        dve.wait_ge(coef_ps, 1)
                        dve.tensor_scalar(coef[:, 0:3], PS[:, 0, 0:3], 1.0 / (F * D), None, ALU.mult).then_inc(coef_out, 1)
                        dve.wait_ge(coef_out, 1)

                    def begin_ffn():
                        weights(0, 0, 2)
                        silu(0, 0)
                        silu(1, 1)

                    links = [0, 0]

                    def link(ins):
                        ins.then_inc(chain, 1)
                        links[1] += 1
                        return links[0] + links[1]

                    def high_x(b, k):
                        dve.wait_ge(xt_in[k % 2], (b * 2 + k // 2 + 1) * 16)
                        dve.tensor_copy(xH[:, k, :], xraw[:, k % 2, :]).then_inc(xhigh, 1)

                    def rope_products(r, use, i):
                        ps, half = g_bank(use[1]), P // 2
                        if i == 0:
                            dve.wait_ge(g_done, use[0] + 1)
                            if not isinstance(r, int) or r:
                                dve.wait_ge(lo_out, r)
                            dve.tensor_tensor(rp[:, 0], ps, cs[:], ALU.mult)
                        elif i == 1:
                            dve.tensor_tensor(rp[0:half, 1], ps[half:P, :], sn[0:half, :], ALU.mult)
                        else:
                            dve.tensor_tensor(rp[half:P, 1], ps[0:half, :], sn[half:P, :], ALU.mult).then_inc(g_free, 1)

                    def maxima(g, n):
                        t, h, m = U1[n]
                        w = P * (t + 1)
                        dve.wait_ge(p1_done, g[0] * NU + n + 1)
                        dve.tensor_reduce(negM[:, h:h + m, t],
                                          PS[:, BANKS_P1[(g[1] * NU + n) % 3], 0:m * w].rearrange("p (m w) -> p m w", m=m),
                                          AX_X, ALU.max, negate=True).then_inc(p1_free, 1)

                    def split_max(g):
                        dve.wait_ge(p1_free, g[0] * NU + NU + 3)
                        a = link(dve.tensor_copy(mp[:, 0], negM[:]))
                        dve.wait_ge(chain, a)
                        a = link(dve.tensor_tensor(negR[:], negM[:], mp[:, 0], ALU.subtract))
                        dve.wait_ge(chain, a)
                        a = link(dve.tensor_copy(mp[:, 1], negR[:]))
                        dve.wait_ge(chain, a)
                        dve.tensor_tensor(mp[:, 2], negR[:], mp[:, 1], ALU.subtract).then_inc(max_split, 1)

                    def max_copy(g, use):
                        dve.wait_ge(g_done, use[0] + 1)
                        dve.wait_ge(max_in, g[0] * 16 + 16)
                        dve.tensor_copy(mT[:], g_bank(use[1]).bitcast(BF16)[0:NM, 0:P]).then_inc(g_free, 1)

                    def turn_copy(half, use):
                        dve.wait_ge(g_done, use[0] + 1)
                        dve.tensor_copy(V[:, :, 4 * half:4 * half + 4, 0:HD],
                                        g_bank(use[1])[:, 0:2 * P].rearrange("p (t h d) -> p t h d", t=QT, d=HD)
                                        ).then_inc(g_free, 1)

                    def add_out(b, t, use):
                        yt = y[:, b * QT + t, :]
                        if t == 0:
                            dve.wait_ge(xn_in, B * 16)
                        dve.wait_ge(g_done, use[0] + 1)
                        dve.tensor_tensor(yt, g_bank(use[1]), yt, ALU.add).then_inc(g_free, 1)

                    def statistics(b, t, use):
                        yt = y[:, b * QT + t, :]
                        hold(dve, g_free, use[0] + 3, passed)
                        a = link(dve.bn_stats(bnst[:, t], yt))
                        hold(dve, chain, a, passed)
                        a = link(dve.bn_aggr(mv[:, t], bnst[:, t]))
                        if t == QT - 1:
                            dve.wait_ge(chain, a)
                            dve.tensor_scalar(mean[:], mv[:, :, 0], -1.0, None, ALU.mult)
                            a = link(dve.tensor_scalar(sd[:], mv[:, :, 1], EPS, None, ALU.add))
                            dve.wait_ge(chain, a)
                            dve.reciprocal(sd[:], sd[:]).then_inc(var_out, 1)

                    def first_tile(r, n):
                        for i in range(3):
                            rope_products(r, (n, n % 2), i)
                        dve.wait_ge(g_free, n + 3)
                        dve.tensor_tensor(rp[:, 0], rp[:, 0], rp[:, 1], ALU.add).then_inc(added, 1)
                        dve.wait_ge(hi_out, r + 1)
                        dve.tensor_tensor(rp[:, 1], rp[:, 0], parts[:, 0], ALU.subtract).then_inc(rest, 1)
                        dve.wait_ge(mid_out, r + 1)
                        dve.tensor_tensor(parts[:, 2], rp[:, 1], parts[:, 1], ALU.subtract).then_inc(lo_out, 1)

                    CH_SECTION = 3 * NKV + 2 * QT + 1
                    CH_FIRST = 2 * KT + 3 * NKV

                    def section(sec):
                        b = sec.b
                        full = sec.prev and sec.nxt
                        if full:
                            links[:] = [b * CH_SECTION + (CH_FIRST - CH_SECTION), 0]
                        elif sec.prev:
                            links[:] = [CH_FIRST + CH_SECTION * (b - 1), 0]
                        for st in range(NKV):
                            g = (b * NKV + st, st) if sec.cur else None
                            t = sec.tile(st, 4)
                            for n in range(NU):
                                if g:
                                    maxima(g, n)
                                if st and n == 0 and sec.use("project", st - 1) and st - 1 in ROPES:
                                    rope_products(ROPES[st - 1] + b * N_ROPE, sec.use("project", st - 1), 2)
                                if st and n == 1 and sec.use("turn", st - 1):
                                    turn_copy(TURN[st - 1], sec.use("turn", st - 1))
                                at = {1: (st - 1, 0), 2: (st - 1, 1)}
                                if st == NKV - 1:
                                    at[4], at[5] = (st, 0), (st, 1)
                                if n in at and sec.use("out", at[n][0]):
                                    of = at[n][0]
                                    (add_out, statistics)[at[n][1]](b - 1, of - OUT_STEP, sec.use("out", of))
                                    if not sec.cur and n == 2 and of < OUT_STEP + 2:
                                        weights(3, 1, of - OUT_STEP)
                                if n == (4 if st == 7 else 3) and sec.use("max", st):
                                    max_copy(sec.behind(st, 1), sec.use("max", st))
                                if n == 4 and t:
                                    dve.wait_ge(den_in, t[0] * 16 + 16)
                                    dve.wait_ge(o_norm, t[0] + 1)
                                    dve.reciprocal(inv[:], den[:]).then_inc(den_inv, 1)
                                if not sec.cur and st < 2 and n in (2, 4, 6, 8):
                                    turned_low(4 * st + n // 2 - 1)
                                if not sec.prev and st == 1 and n in (2, 4, 6, 8):
                                    k = n // 2 - 1
                                    a = link(dve.tensor_copy(woH[:, k], raw_o[:, k]))
                                    dve.wait_ge(chain, a)
                                    dve.tensor_tensor(woL[:, k], raw_o[:, k], woH[:, k].bitcast(F32), ALU.subtract
                                                      ).then_inc(wsplit, 1)
                                if sec.nxt and (st, n) in SPLIT_X:
                                    for k in SPLIT_X[st, n]:
                                        high_x(b + 1, k)
                                use = sec.use("project", st)
                                if n in (9, 10) and use and st in ROPES:
                                    rope_products(ROPES[st] + b * N_ROPE, use, n - 9)
                                if n == 9 and use and st not in ROPES:
                                    dve.wait_ge(g_done, use[0] + 1)
                                    dve.tensor_copy(vT[:], g_bank(use[1])).then_inc(g_free, 1)
                            if g:
                                split_max(g)
                            if not sec.cur and st == 0:
                                coefficients()
                            if not sec.cur and st == 1:
                                means()
                            if not sec.cur and st == 2:
                                for n in range(2 * KT, 3 * KT):
                                    if n % 2 == 0:
                                        weights(0, 0, n // 2 - KT)
                                    turned_low(n)
                            if not sec.cur and st == 3:
                                begin_ffn()
                            if st == NKV - 1 and sec.prev:
                                dve.wait_ge(std_out, b)
                                for t in (2, 3):
                                    yt = y[:, (b - 1) * QT + t, :]
                                    dve.tensor_scalar(yt, yt, mv[:, t, 0:1], rs[:, t:t + 1], ALU.subtract,
                                                      ALU.mult).then_inc(x1_out, 1)
                        assert not full or links[1] == CH_SECTION

                    dve.memset(V[:], 1.0).then_inc(ready0, 1)
                    dve.memset(Ks[:], 1.0).then_inc(ready0, 1)
                    dve.memset(mp_all[:], 0.0).then_inc(ready0, 1)
                    dve.memset(onesf[:], 1.0).then_inc(ready0, 1)
                    for ring in (g_free, exped, pv_done, co_abs, h_out):
                        dve.sem_inc(ring, 2)
                    for ring, free in ((p1_free, 3), (o_out, 1), (o_norm, 1), (o_kept, 16), (max_in, 16), (o_split, 4),
                                       (y_free, 16)):
                        dve.sem_inc(ring, free)
                    for k in range(KT):
                        high_x(0, k)
                        dve.wait_ge(wq_in[k], 16)
                        a = link(dve.tensor_copy(wqH[:, k], raw_q[:, k]))
                        dve.wait_ge(chain, a)
                        dve.tensor_tensor(wqL[:, k], raw_q[:, k], wqH[:, k].bitcast(F32), ALU.subtract).then_inc(wsplit, 1)
                    dve.wait_ge(raw_in, 6 * 16)
                    dve.wait_ge(wsplit, KT)
                    for n, (_, r) in enumerate(FIRST):
                        first_tile(r, n)
                    sections(Run(dve, section))
                    pair(0, True, False)
                    with dve.Fori(1, PAIRS - 1) as it:
                        pair(it, False, False)
                    pair(PAIRS - 1, False, True)

                @block.tensor
                def _(pe):
                    def three(dst, stH, stL, moH, moL, k, n):
                        pe.matmul(dst, stH, moH, start=(k == 0), stop=False)
                        pe.matmul(dst, stH, moL, start=False, stop=False)
                        return pe.matmul(dst, stL, moH, start=False, stop=(k == n - 1))

                    def gate_up(n, n3, par, wpar, b):
                        pe.wait_ge(h_out, n + 1)
                        for t in range(2):
                            pe.wait_ge(w_out, n3 + t + 1)
                            for k in range(KT):
                                c = slice(P * k, P * (k + 1))
                                m = three(PS[:, 2 * par + t, :], WH[wpar][:, t, c], WL[wpar][:, t, c],
                                          XH[:, k, b, :], XL[:, k, b, :], k, KT)
                            m.then_inc(gu_done, 1)

                    def down(n, n3, par, wpar):
                        pe.wait_ge(h_out, n + 3)
                        pe.wait_ge(w_out, n3 + 3)
                        for t in range(QT):
                            pe.wait_ge(y_free, n * QT + t + 13)
                            c = slice(P * t, P * (t + 1))
                            three(PS[:, BANK_Y + t, :], hH[:, par, c], hL[:, par, c], WH[wpar][:, 2], WL[wpar][:, 2],
                                  0, 1).then_inc(y_done, 1)

                    def pair(it, first, last):
                        for u in range(UNITS):
                            i, n, v = u // B, it * UNITS + u, u + 1
                            if first and u == 0:
                                pass
                            elif v < UNITS:
                                if first and v == B - 1:
                                    turn_last()
                                gate_up(n + 1, it * 6 + 3 * (v // B), v % 2, v // B, v % B)
                            elif not last:
                                gate_up(n + 1, it * 6 + 6, 0, 0, 0)
                            down(n, it * 6 + 3 * i, u % 2, i)

                    def turn_x1(n):
                        k, b = n % KT, n // KT
                        for t in range(QT):
                            m = pe.transpose(PS[:, turn_bank(n), P * t:P * (t + 1)], y[:, b * QT + t, P * k:P * (k + 1)],
                                             idf[:])
                        m.then_inc(t_done, 1)

                    def turn_early(n):
                        if n >= 2:
                            pe.wait_ge(t_out, n - 1)
                        turn_x1(n)

                    def turn_last():
                        pe.wait_ge(h_out, 4)
                        pe.wait_ge(x1_out, B * QT)
                        for n in range((B - 1) * KT, B * KT):
                            pe.wait_ge(t_out, n - 1)
                            turn_x1(n)
                        pe.wait_ge(t_out, B * KT)

                    def begin_ffn():
                        pe.wait_ge(t_out, (B - 1) * KT)
                        gate_up(0, 0, 0, 0, 0)
                        pe.wait_ge(exped, B * NKV * NU + 2)
                        gate_up(1, 0, 1, 0, 1)

                    def project(b, tile, use, k):
                        if k == 0:
                            pe.wait_ge(g_free, use[0] + 1)
                        pe.wait_ge(xsplit, b * KT + k + 1)
                        c = slice(P * tile, P * (tile + 1))
                        m = three(g_bank(use[1]), wqH[:, k, c], wqL[:, k, c], xH[:, k], xL[:, k], k, KT)
                        if k == KT - 1:
                            m.then_inc(g_done, 1)

                    def turn(half, use, v_use):
                        hold(pe, g_free, use[0] + 1, passed)
                        hold(pe, g_free, v_use + 3, passed)
                        rows = slice(64 * half, 64 * half + 64)
                        for t in range(QT):
                            m = pe.transpose(g_bank(use[1])[:, 64 * t:64 * (t + 1)], vT[rows, P * t:P * (t + 1)],
                                             idf[rows, rows])
                        m.then_inc(g_done, 1)

                    def pass1(g, n):
                        t, h0, m = U1[n]
                        w = P * (t + 1)
                        bank = PS[:, BANKS_P1[(g[1] * NU + n) % 3], :]
                        pe.wait_ge(p1_free, g[0] * NU + n + (3 if g[1] + n == 0 else 1))
                        for i in range(m):
                            pe.matmul(bank[:, i * w:(i + 1) * w], Qs[0:ROWS, GH * g[1] + h0 + i, P * t:P * (t + 1)],
                                      Ks[0:ROWS, g[1], 0:w], start=True, stop=False)
                            last = pe.matmul(bank[:, (i + 1) * w - P:(i + 1) * w], idb[:], mk[:], start=False, stop=True)
                        last.then_inc(p1_done, 1)

                    def max_transpose(g, use):
                        pe.wait_ge(max_split, g[0] + 1)
                        pe.wait_ge(g_free, use[0] + 1)
                        pe.transpose(g_bank(use[1]).bitcast(BF16)[:, 0:P], mp_all[:], idb[:]).then_inc(g_done, 1)

                    def pass2(g, n):
                        t, h0, m = U2[n]
                        w = S - P * t
                        bank = PS[:, BANK_P2 + (g[1] * NU + n) % 2, :]
                        pe.wait_ge(exped, g[0] * NU + n + 1)
                        if n == 0:
                            pe.wait_ge(max_in, g[0] * 16 + 32)
                        for i in range(m):
                            pe.matmul(bank[:, i * w:(i + 1) * w], Ks[0:ROWS + 3, g[1], P * t:P * (t + 1)],
                                      Qs[0:ROWS + 3, GH * g[1] + h0 + i, P * t:S], start=True, stop=False)
                            last = pe.matmul(bank[:, i * w:i * w + P], mk[:], idb[:], start=False, stop=True)
                        last.then_inc(p2_done, 1)

                    def pv(g, t):
                        if t == 0:
                            pe.wait_ge(o_out, g[0] + 1)
                        pe.wait_ge(exped, g[0] * NU + LAST2[t] + 3)
                        for h in range(GH):
                            last = pe.matmul(PS[32 * h:32 * (h + 1), BANK_O, P * t:S], V[:, t, g[1], :],
                                             Pt[:, t % 2, h, P * t:S], start=(t == 0), stop=(t == QT - 1),
                                             tile_position=(0, 32 * h))
                        last.then_inc(pv_done, 1)

                    def project_out(b, t, use, k):
                        if k == 0:
                            pe.wait_ge(g_free, use[0] + 1)
                            if t == 0:
                                pe.wait_ge(wsplit, 2 * KT)
                        pe.wait_ge(o_split, b * KT + k + 5)
                        c = slice(P * t, P * (t + 1))
                        m = three(g_bank(use[1]), OH[:, k, c], OL[:, k, c], woH[:, k], woL[:, k], k, KT)
                        if k == KT - 1:
                            m.then_inc(g_done, 1)

                    def section(sec):
                        b = sec.b
                        for st in range(NKV):
                            if sec.cur:
                                if st % 2 == 0:
                                    pe.wait_ge(q_in[st // 2], (b + 1) * 96)
                                if st == 0:
                                    pe.wait_ge(k_in[0], (b + 1) * 96)
                                elif st == 4 and sec.prev:
                                    pe.wait_ge(k_in[1], b * 96)
                            g2, g3 = sec.behind(st, LAG), sec.behind(st, LAG + 1)
                            g1 = (b * NKV + st, st) if sec.cur else None
                            up, out_use = sec.use("project", st), sec.use("out", st)
                            for n in range(NU):
                                if g1:
                                    pass1(g1, n)
                                if g2:
                                    pass2(g2, n)
                                if n == 0 and g3:
                                    pv(g3, 2)
                                if n == 2 and g3:
                                    pv(g3, 3)
                                if n in PROJECT_AT and up:
                                    tile, who = PROJECT[st]
                                    project(b + (who == "nxt"), tile, up, PROJECT_AT.index(n))
                                if not sec.cur and st < 2 and n in (2, 4, 6, 8):
                                    m = 4 * st + n // 2 - 1
                                    if m == 0:
                                        pe.wait_ge(p1_free, B * NKV * NU + 3)
                                        pe.wait_ge(x1_out, (B - 1) * QT)
                                    turn_early(m)
                                if n == 6 and g2:
                                    pv(g2, 0)
                                if n == 9 and g2:
                                    pv(g2, 1)
                                if n == 9 and sec.use("turn", st):
                                    v_use = sec.use("project", 0)[0]
                                    turn(TURN[st], sec.use("turn", st), v_use)
                                if out_use:
                                    for k in ({1: (0,), 2: (1,), 3: (2, 3)} if st == 7 else {7: (0,), 9: (1,), 10: (2, 3)}
                                              ).get(n, ()):
                                        project_out(b - 1, st - OUT_STEP, out_use, k)
                                if n == 3 and sec.use("max", st):
                                    max_transpose(sec.behind(st, 1), sec.use("max", st))
                            if not sec.cur and st == 1:
                                pe.wait_ge(fchain, 1)
                                pe.wait_ge(t_out, 2 * KT)
                                pe.matmul(PS[:, 0, 0:3], onesf[:], csum[:, 0:3], start=True, stop=True).then_inc(coef_ps, 1)
                            if not sec.cur and st == 2:
                                pe.wait_ge(coef_out, 1)
                                for n in range(2 * KT, 3 * KT):
                                    turn_early(n)
                            if not sec.cur and st == 3:
                                begin_ffn()

                    pe.wait_ge(ready0, 4)
                    for k in range(KT):
                        pe.wait_ge(wsplit, k + 1)
                        for n in range(2):
                            project(0, FIRST[n][0], (n, n % 2), k)
                    for k in range(KT):
                        project(0, FIRST[2][0], (2, 0), k)
                    sections(Run(pe, section))
                    pe.wait_ge(o_out, B * NKV + 1)
                    last_use = Section(B, True, False, False).use("out", NKV - 1)[0]
                    pe.wait_ge(g_free, last_use + 3)
                    pair(0, True, False)
                    with pe.Fori(1, PAIRS - 1) as it:
                        pair(it, False, False)
                    pair(PAIRS - 1, False, True)


def lay_out(a):
    x = a["L0_attn_hidden_states"]
    xt = x.transpose(0, 2, 1).reshape(B, KT, P, S).transpose(0, 2, 1, 3)
    xn = x.reshape(B, QT, P, D).transpose(0, 2, 1, 3)
    wq = a["L0_attn_Wq"].reshape(QT, 8, HD, D).transpose(0, 2, 1, 3).reshape(NH * HD, D)
    wk = a["L0_attn_Wk"].reshape(NKV, HD, D).transpose(1, 0, 2).reshape(NKV * HD, D)
    w = np.concatenate([wq, wk, a["L0_attn_Wv"]], axis=0)
    wqkv = w.T.reshape(KT, P, -1).transpose(1, 0, 2)
    wo = a["L0_attn_Wo"].T.reshape(KT, P, D).transpose(1, 0, 2)

    def up(w):
        return w.reshape(NT, P, KT, P).transpose(0, 3, 2, 1).reshape(NT, P, D)

    def down(w):
        return w.T.reshape(NT, P, D)

    pairs = [(up, "w1"), (up, "w3"), (down, "w2")]
    wall = np.stack([np.stack([f(a[f"L0_ffn_{n}"]), f(a[f"L0_ffn_mean_{n}"])], axis=2) for f, n in pairs])
    return {"xt": xt, "x": xn, "wqkv": wqkv, "wo": wo, "wall": wall}


def constants():
    inv = (1.0 / 10000.0 ** (np.arange(0, HD, 2, dtype=np.float32) / HD)).astype(np.float32)
    ang = np.outer(np.arange(S, dtype=np.float32), inv).astype(np.float32)
    rows = np.repeat(ang.T, 8, axis=0)
    cos = np.concatenate([np.cos(rows), np.cos(rows)], axis=0)
    sin = np.concatenate([-np.sin(rows), np.sin(rows)], axis=0)
    return {"cos": cos.astype(np.float32), "sin": sin.astype(np.float32),
            "ident": np.eye(P, dtype=np.float32).astype(mybir.dt.np(BF16)), "identf": np.eye(P, dtype=np.float32),
            "mask": np.where(np.tri(P, dtype=bool), np.float32(0), np.float32(MASKED)).astype(mybir.dt.np(BF16))}


_ORDER = ("xt", "x", "wqkv", "wo", "wall", "cos", "sin", "ident", "identf", "mask")


def kernel(**inputs):
    from concourse import bacc
    from concourse.bass_utils import run_bass_kernel_spmd

    arrays = {**lay_out({k: np.asarray(v) for k, v in inputs.items()}), **constants()}
    arrays = {k: np.ascontiguousarray(arrays[k]) for k in _ORDER}
    nc = bacc.Bacc("TRN2", target_bir_lowering=False, num_devices=1)
    args = [nc.dram_tensor(k, a.shape, mybir.dt.from_np(a.dtype), kind="ExternalInput").ap() for k, a in arrays.items()]
    out = nc.dram_tensor("out", (B, P, QT, D), F32, kind="ExternalOutput").ap()
    layer(nc, *args, out)
    r = run_bass_kernel_spmd(nc, [arrays], core_ids=[0])
    return r.results[0]["out"].transpose(0, 2, 1, 3).reshape(B, S, D)
```
